# Optimizing a Trainium2 kernel written in Bass

```python
import numpy as np
import jax
import jax.numpy as jnp

def _softmax(x, axis=-1):
    return jax.nn.softmax(x, axis=axis)

def _gelu(x):
    return jax.nn.gelu(x, approximate=True)

def _silu(x):
    return jax.nn.silu(x)

def _sigmoid(x):
    return jax.nn.sigmoid(x)

def _layernorm(x, axis=-1, eps=1e-05):
    m = jnp.mean(x, axis=axis, keepdims=True)
    v = jnp.var(x, axis=axis, keepdims=True)
    return (x - m) / jnp.sqrt(v + eps)

def _scatter_add(tgt, idx, src, axis=0):
    return tgt.at[idx].add(src)

def _segment_sum(src, seg, n):
    return jax.ops.segment_sum(src, seg, n)
kernel_name = 'mk_seq_preln_d1_jaxref_r8_678c91'

def setup_inputs(seed: int=0):
    np.random.seed(seed)
    _w = jnp.asarray

    def _L0_attn_setup():
        import jax, jax.numpy as jnp
        import numpy as np
        N_HEAD = 16
        PAGE_SIZE = 32
        ROPE_THETA = 10000.0

        def _rope_tables(T, D, dtype):
            inv = 1.0 / ROPE_THETA ** (np.arange(0, D, 2, dtype=np.float32) / D)
            ang = np.outer(np.arange(T, dtype=np.float32), inv)
            return (jnp.asarray(np.cos(ang), dtype), jnp.asarray(np.sin(ang), dtype))

        def _apply_rope(x, cos, sin):
            x1 = x[..., 0::2]
            x2 = x[..., 1::2]
            c = cos[None, :, None, :]
            s = sin[None, :, None, :]
            out = jnp.stack([x1 * c - x2 * s, x1 * s + x2 * c], axis=-1)
            return out.reshape(x.shape)
        key = jax.random.key(seed)
        ks = jax.random.split(key, 6)
        B, T, E = (2, 256, 128)
        L = E // 2
        sc = lambda fan: 1.0 / np.sqrt(fan)
        return {'x': jax.random.normal(ks[0], (B, T, E), jnp.float32), 'wq': jax.random.normal(ks[1], (E, E), jnp.float32) * sc(E), 'w_down': jax.random.normal(ks[2], (E, L), jnp.float32) * sc(E), 'wk_up': jax.random.normal(ks[3], (L, E), jnp.float32) * sc(L), 'wv_up': jax.random.normal(ks[4], (L, E), jnp.float32) * sc(L), 'wo': jax.random.normal(ks[5], (E, E), jnp.float32) * sc(E)}
    _L0_attn_in = _L0_attn_setup()

    def _L0_ffn_setup():
        import jax, jax.numpy as jnp
        import numpy as np
        TOP_K = 2
        NUM_EXPERTS = 8
        DIM = 128
        HIDDEN = 352
        BS, SLEN = (2, 128)

        def _grouped_ffn(x, w1, w2, w3, counts):
            num_experts = w1.shape[0]
            ends = jnp.cumsum(counts)
            starts = ends - counts
            t = jnp.arange(x.shape[0])
            out = jnp.zeros((x.shape[0], w2.shape[-1]), x.dtype)
            for e in range(num_experts):
                m = ((t >= starts[e]) & (t < ends[e])).astype(x.dtype)[:, None]
                xe = x * m
                h = jax.nn.silu(xe @ w1[e]) * (xe @ w3[e])
                out = out + h @ w2[e] * m
            return out
        key = jax.random.key(seed)
        k = jax.random.split(key, 5)
        std = 0.02
        return {'x': jax.random.normal(k[0], (BS, SLEN, DIM), jnp.float32), 'gate_w': jax.random.normal(k[1], (NUM_EXPERTS, DIM), jnp.float32) * std, 'expert_bias': jnp.zeros((NUM_EXPERTS,), jnp.float32), 'w1': jax.random.normal(k[2], (NUM_EXPERTS, DIM, HIDDEN), jnp.float32) * std, 'w2': jax.random.normal(k[3], (NUM_EXPERTS, HIDDEN, DIM), jnp.float32) * std, 'w3': jax.random.normal(k[4], (NUM_EXPERTS, DIM, HIDDEN), jnp.float32) * std}
    _L0_ffn_in = _L0_ffn_setup()
    _d = {'L0_attn_x': _L0_attn_in['x'], 'L0_attn_wq': _L0_attn_in['wq'], 'L0_attn_w_down': _L0_attn_in['w_down'], 'L0_attn_wk_up': _L0_attn_in['wk_up'], 'L0_attn_wv_up': _L0_attn_in['wv_up'], 'L0_attn_wo': _L0_attn_in['wo'], 'L0_ffn_gate_w': _L0_ffn_in['gate_w'], 'L0_ffn_expert_bias': _L0_ffn_in['expert_bias'], 'L0_ffn_w1': _L0_ffn_in['w1'], 'L0_ffn_w2': _L0_ffn_in['w2'], 'L0_ffn_w3': _L0_ffn_in['w3']}
    _x0 = _d['L0_attn_x']
    _d['L0_attn_x'] = jax.random.normal(jax.random.fold_in(jax.random.key(seed), 1), (4, 512, 128), dtype=_x0.dtype)
    del _x0
    return _d

def reference(L0_attn_x, L0_attn_wq, L0_attn_w_down, L0_attn_wk_up, L0_attn_wv_up, L0_attn_wo, L0_ffn_gate_w, L0_ffn_expert_bias, L0_ffn_w1, L0_ffn_w2, L0_ffn_w3):

    def _L0_attn_ref(x, wq, w_down, wk_up, wv_up, wo):
        import jax, jax.numpy as jnp
        import numpy as np
        N_HEAD = 16
        PAGE_SIZE = 32
        ROPE_THETA = 10000.0

        def _rope_tables(T, D, dtype):
            inv = 1.0 / ROPE_THETA ** (np.arange(0, D, 2, dtype=np.float32) / D)
            ang = np.outer(np.arange(T, dtype=np.float32), inv)
            return (jnp.asarray(np.cos(ang), dtype), jnp.asarray(np.sin(ang), dtype))

        def _apply_rope(x, cos, sin):
            x1 = x[..., 0::2]
            x2 = x[..., 1::2]
            c = cos[None, :, None, :]
            s = sin[None, :, None, :]
            out = jnp.stack([x1 * c - x2 * s, x1 * s + x2 * c], axis=-1)
            return out.reshape(x.shape)
        B, T, E = x.shape
        H = N_HEAD
        D = E // H
        q = (x @ wq).reshape(B, T, H, D)
        lat = x @ w_down
        k = (lat @ wk_up).reshape(B, T, H, D)
        v = (lat @ wv_up).reshape(B, T, H, D)
        cos, sin = _rope_tables(T, D, x.dtype)
        q = _apply_rope(q, cos, sin)
        k = _apply_rope(k, cos, sin)
        scale = 1.0 / jnp.sqrt(jnp.asarray(D, x.dtype))
        scores = jnp.einsum('bqhd,bkhd->bhqk', q, k) * scale
        pages = jnp.arange(T) // PAGE_SIZE
        allowed = pages[None, :] <= pages[:, None]
        scores = jnp.where(allowed[None, None], scores, jnp.finfo(scores.dtype).min)
        attn = jax.nn.softmax(scores, axis=-1)
        out = jnp.einsum('bhqk,bkhd->bqhd', attn, v).reshape(B, T, E)
        return out @ wo

    def _L0_ffn_ref(x, gate_w, expert_bias, w1, w2, w3):
        import jax, jax.numpy as jnp
        import numpy as np
        TOP_K = 2
        NUM_EXPERTS = 8
        DIM = 128
        HIDDEN = 352
        BS, SLEN = (2, 128)

        def _grouped_ffn(x, w1, w2, w3, counts):
            num_experts = w1.shape[0]
            ends = jnp.cumsum(counts)
            starts = ends - counts
            t = jnp.arange(x.shape[0])
            out = jnp.zeros((x.shape[0], w2.shape[-1]), x.dtype)
            for e in range(num_experts):
                m = ((t >= starts[e]) & (t < ends[e])).astype(x.dtype)[:, None]
                xe = x * m
                h = jax.nn.silu(xe @ w1[e]) * (xe @ w3[e])
                out = out + h @ w2[e] * m
            return out
        bs, slen, dim = x.shape
        num_experts = gate_w.shape[0]
        xf = x.reshape(bs * slen, dim)
        scores = jax.nn.softmax((xf @ gate_w.T).astype(jnp.float32), axis=-1)
        _, sel = jax.lax.top_k(scores + expert_bias, TOP_K)
        top_scores = jnp.take_along_axis(scores, sel, axis=1).reshape(-1)
        sel_flat = sel.reshape(-1)
        counts = jnp.zeros((num_experts,), jnp.int32).at[sel_flat].add(1)
        order = jnp.argsort(sel_flat, stable=True)
        top_scores_sorted = top_scores[order]
        token_idx = order // TOP_K
        routed = xf[token_idx] * top_scores_sorted[:, None].astype(xf.dtype)
        routed_out = _grouped_ffn(routed, w1, w2, w3, counts)
        out = jnp.zeros_like(xf).at[token_idx].add(routed_out)
        return out.reshape(bs, slen, dim)
    x = L0_attn_x
    x = x + _L0_attn_ref(_layernorm(x, axis=-1), L0_attn_wq, L0_attn_w_down, L0_attn_wk_up, L0_attn_wv_up, L0_attn_wo)
    x = x + _L0_ffn_ref(_layernorm(x, axis=-1), L0_ffn_gate_w, L0_ffn_expert_bias, L0_ffn_w1, L0_ffn_w2, L0_ffn_w3)
    return x

_drawn_inputs = setup_inputs


def setup_inputs(seed=0):
    import zlib

    import numpy as np

    out = dict(_drawn_inputs(seed))
    spreads = {'L0_ffn_expert_bias': (0.0, 0.8)}
    factors = {'L0_ffn_gate_w': 8.0, 'L0_ffn_w1': 8.0, 'L0_ffn_w2': 8.0, 'L0_ffn_w3': 8.0}
    for name, (base, spread) in spreads.items():
        noise = np.random.default_rng([zlib.crc32(name.encode()), seed]).standard_normal(out[name].shape)
        drawn = base * np.exp(spread * noise) if base else spread * noise
        out[name] = jnp.asarray(drawn.astype(out[name].dtype))
    for name, factor in factors.items():
        out[name] = (out[name] * factor).astype(out[name].dtype)
    return out
```

```python
from contextlib import ExitStack

import numpy as np

import concourse.bass as bass
from concourse import mybir

F32 = mybir.dt.float32
BF16 = mybir.dt.bfloat16
U32 = mybir.dt.uint32
ALU = mybir.AluOpType
ACT = mybir.ActivationFunctionType
AXX = mybir.AxisListType.X

P = 128
NB, T, E = 4, 512, 128
H = 16
D = E // H
L = E // 2
PAGE = 32
NPAGE = T // PAGE
QT = T // P
NT = NB * QT
EPS = 1e-5
SCALE = 1.0 / float(np.sqrt(D))

PARTS = 3
MASK_ROW = PARTS * PARTS * D
SHIFT_ROW = MASK_ROW + NPAGE
ROWS = SHIFT_ROW + PARTS
BIG = 2.0 ** 126

SR = PARTS * H * QT // 2

HG = 4
NHG = H // HG
AUG = 32

NE, HID = 8, 352
HJ = [(0, 128), (128, 128), (256, 96)]

MAX_UNITS = ([(3, h, 1) for h in range(H)] + [(2, h, 1) for h in range(H)]
             + [(1, h, 2) for h in range(0, H, 2)] + [(0, h, 4) for h in range(0, H, 4)])
NMU = len(MAX_UNITS)
NG = NHG * QT
NPAIR = 2 * NG


def constants():
    bf = mybir.dt.np(BF16)
    inv = 1.0 / 10000.0 ** (np.arange(0, D, 2, dtype=np.float32) / D)
    ang = np.outer(np.arange(T, dtype=np.float32), inv)
    cos, sin = np.cos(ang).astype(np.float32).T, np.sin(ang).astype(np.float32).T
    rope = np.empty((D, H, 2, T), np.float32)
    for d in range(D):
        rope[d, :, 0] = cos[d // 2]
        rope[d, :, 1] = sin[d // 2] if d % 2 else -sin[d // 2]
    page = np.arange(T) // PAGE
    rows = np.arange(NPAGE)[:, None]
    k_rows = np.concatenate([(page[None] == rows), np.ones((PARTS, T))]).astype(np.float32)
    q_rows = np.where(page[None] < rows, -BIG, 0.0).astype(np.float32)
    return {
        "c_rope": rope.reshape(P, 2 * T),
        "c_krows": k_rows.astype(bf),
        "c_qrows": q_rows.astype(bf),
        "c_eye": np.eye(P, dtype=np.float32),
        "c_eye16": np.eye(P).astype(bf),
        "c_expert": np.tile(np.arange(NE, dtype=np.float32), (P, 1)),
    }


def build_block(nc, x, wq, w_down, wk_up, wv_up, wo, gate_w, expert_bias, w1, w2, w3, out,
                c_rope, c_krows, c_qrows, c_eye, c_eye16, c_expert):
    ds = bass.ds
    with ExitStack() as ctx:
        def sb(name, shape, dt=F32):
            return ctx.enter_context(nc.sbuf_tensor(name, shape, dt))

        def ps(name, shape, dt=F32):
            return ctx.enter_context(nc.psum_tensor(name, shape, dt))

        def sem(name):
            return ctx.enter_context(nc.semaphore(name))

        parts_dram = nc.dram_tensor("parts_dram", (NB, 2, PARTS, P, T), BF16, kind="Internal").ap()
        shift_dram = nc.dram_tensor("shift_dram", (NB, PARTS * H * QT, P), BF16, kind="Internal").ap()
        heads_dram = nc.dram_tensor("heads_dram", (NB, NHG * P, T), F32, kind="Internal").ap()

        stack = sb("stack", [P, 2, NB, H * T], BF16)
        q_stack, k_stack = stack[:, 0], stack[:, 1]
        x_sb = sb("x_sb", [P, NT, E])
        numer = sb("numer", [P, NT * E])
        v_all = sb("v_all", [P, NT, E])
        v_aug = sb("v_aug", [P, QT, H, AUG])
        work = sb("work", [P, 8 * T])
        rope = sb("rope", [P, 2, T])
        parts = sb("parts", [P, 2, PARTS, T], BF16)
        xT = sb("xT", [P, T])
        heads_sb = sb("heads_sb", [P, 2, T])
        w_raw = sb("w_raw", [P, 4, E])
        wd_sb = sb("wd_sb", [P, L])
        wdT = sb("wdT", [L, E])
        w_proj = sb("w_proj", [P, 5, E])
        eye = sb("eye", [P, P])
        eye16 = sb("eye16", [P, P], BF16)
        stats = sb("stats", [P, NT, 6])
        moments = sb("moments", [P, NT, 2])
        rstd = sb("rstd", [P, NT])
        negmax = sb("negmax", [P, H * QT])
        shift_rest = sb("shift_rest", [P, H * QT])
        shift = sb("shift", [P, PARTS, H * QT], BF16)
        shiftT = sb("shiftT", [SR, 2, P], BF16)
        gw_sb = sb("gw_sb", [NE, E])
        gwT = sb("gwT", [P, NE])
        bias_sb = sb("bias_sb", [P, NE])
        expert_no = sb("expert_no", [P, NE])

        rot = work[:, 0:4 * T].rearrange("p (w k t) -> p w k t", w=2, k=2)
        rotated = work[:, 4 * T:6 * T].rearrange("p (w t) -> p w t", w=2)
        rest = work[:, 6 * T:8 * T].rearrange("p (w t) -> p w t", w=2)
        prob = work[:, :].rearrange("p (s g t) -> p s g t", s=2, g=HG)
        area = stack[:, :, :, :].rearrange("p w b n -> p (w b n)").bitcast(F32)
        SEQ = H * T // 2
        denom = area[:, 0:NB * T]
        w13 = area[:, NB * T:NB * T + NE * 2 * HID].rearrange("p (e w n) -> p e w n", e=NE, w=2)
        assert NB * T + NE * 2 * HID <= 2 * SEQ
        k_area = area[:, NB * SEQ:]
        w2_sb = k_area[:, 0:NE * 3 * E].rearrange("p (e j n) -> p e j n", e=NE, j=3)
        assert NE * 3 * E <= SEQ
        xn = numer[:, 0:QT * E].rearrange("p (t e) -> p t e", e=E)
        xn2 = v_all
        xn2T = k_area[:, SEQ:SEQ + NT * P]
        route = k_area[:, SEQ + NT * P:SEQ + NT * P + 12 * NT * NE].rearrange("p (k t e) -> p k t e", k=12, t=NT)
        assert NT * P + 12 * NT * NE <= SEQ
        weight = route[:, 11].rearrange("p t e -> p (t e)")
        gate = work[:, 0:2 * HID].rearrange("p (s n) -> p s n", s=2)
        hid = work[:, 2 * HID:4 * HID].rearrange("p (s n) -> p s n", s=2)
        hidT = work[:, 4 * HID:4 * HID + 6 * P].rearrange("p (s n) -> p s n", s=2)
        stage = work[:, 4 * HID + 6 * P:4 * HID + 8 * P].rearrange("p (s n) -> p s n", s=2)
        y_sb = work[:, 4 * HID + 8 * P:4 * HID + 10 * P].rearrange("p (s n) -> p s n", s=2)
        assert 4 * HID + 10 * P <= 8 * T

        ps_a = ps("ps_a", [P, 2, T])
        ps_b = ps("ps_b", [P, 4, T])
        ps_o = ps("ps_o", [P, T])
        ps_m = ps("ps_m", [P, T])
        ps_b2 = ps_b[:, :, :].rearrange("p (s w) t -> p s w t", s=2)
        shiftT_ps = ps_m[0:SR, 0:P].bitcast(BF16).rearrange("p (k q) -> p k q", k=2)
        shift_cols = shift[:, :, :].rearrange("p k c -> p (k c)")

        x_loaded = [sem(f"x_loaded{b}") for b in range(NB)]
        w_loaded = sem("w_loaded")
        c_loaded = sem("c_loaded")
        rows_loaded = sem("rows_loaded")
        stats_done, moments_done, var_done = sem("stats_done"), sem("moments_done"), sem("var_done")
        std_done, rstd_done, xn_ready = sem("std_done"), sem("rstd_done"), sem("xn_ready")
        wdT_ps, wdT_done, wkv_ps, w_ready = sem("wdT_ps"), sem("wdT_done"), sem("wkv_ps"), sem("w_ready")
        xT_ps, xT_copied = sem("xT_ps"), sem("xT_copied")
        proj_done, rope_read = sem("proj_done"), sem("rope_read")
        v_ps, v_copied = sem("v_ps"), sem("v_copied")
        rope_added = [sem("q_rotated"), sem("k_rotated")]
        split_step = sem("split_step")
        parts_ready = [sem("q_parts_ready"), sem("k_parts_ready")]
        parts_saved = [sem("q_parts_saved"), sem("k_parts_saved")]
        stack_loaded = sem("stack_loaded")
        max_scores, max_read = sem("max_scores"), sem("max_read")
        shift_step, shift_ready = sem("shift_step"), sem("shift_ready")
        shiftT_done, shiftT_copied = sem("shiftT_done"), sem("shiftT_copied")
        shift_saved, shift_loaded = sem("shift_saved"), sem("shift_loaded")
        aug_filled, v_aug_ready = sem("aug_filled"), sem("v_aug_ready")
        scores_ready, exp_done, pv_done = sem("scores_ready"), sem("exp_done"), sem("pv_done")
        heads_copied = sem("heads_copied")
        heads_saved = [sem("heads_saved0"), sem("heads_saved1")]
        sums_loaded = [sem(f"sums_loaded{b}") for b in range(NB)]
        w13_loaded, w2_loaded, g_loaded = sem("w13_loaded"), sem("w2_loaded"), sem("g_loaded")
        inv_done, normed, wo_done, x2_ready = sem("inv_done"), sem("normed"), sem("wo_done"), sem("x2_ready")
        stats2_done, moments2_done, var2_done = sem("stats2_done"), sem("moments2_done"), sem("var2_done")
        std2_done, rstd2_done, xn2_ready = sem("std2_done"), sem("rstd2_done"), sem("xn2_ready")
        gwT_ps, gwT_done = sem("gwT_ps"), sem("gwT_done")
        xn2T_ps, xn2T_copied, logits_done = sem("xn2T_ps"), sem("xn2T_copied"), sem("logits_done")
        route_step, gate_exp = sem("route_step"), sem("gate_exp")
        staged = [sem("staged0"), sem("staged1")]
        up_done, gate_done, hid_done = sem("up_done"), sem("gate_done"), sem("hid_done")
        hidT_ps, hidT_copied, hidT_copied2, down_done = sem("hidT_ps"), sem("hidT_copied"), sem("hidT_copied2"), sem("down_done")
        y_ready = sem("y_ready")
        y_saved = [sem("y_saved0"), sem("y_saved1")]

        block = ctx.enter_context(nc.Block())

        x_tiles = x.rearrange("b (t p) e -> p (b t) e", p=P)
        out_tiles = out.rearrange("b (t p) e -> p (b t) e", p=P)

        @block.sync
        def _(sp):
            for b in range(NB):
                sp.dma_start(x_sb[:, QT * b:QT * (b + 1), :], x_tiles[:, QT * b:QT * (b + 1), :]).then_inc(x_loaded[b], 16)
            for b in range(NB):
                sp.dma_start(q_stack[MASK_ROW:SHIFT_ROW, b, :].rearrange("p (h t) -> p h t", h=H),
                             c_qrows.unsqueeze(1).to_broadcast([NPAGE, H, T])).then_inc(rows_loaded, 16)
                sp.dma_start(k_stack[MASK_ROW:ROWS, b, :].rearrange("p (h t) -> p h t", h=H),
                             c_krows.unsqueeze(1).to_broadcast([NPAGE + PARTS, H, T])).then_inc(rows_loaded, 16)

            with sp.Fori(0, NB) as b:
                for w in range(2):
                    sp.wait_ge(parts_ready[w], b + 1)
                    sp.dma_start(parts_dram[b, w].rearrange("k p t -> p k t"), parts[:, w]).then_inc(parts_saved[w], 16)
                sp.wait_ge(stack_loaded, b * STACK_DMAS)
                for w in range(2):
                    sp.wait_ge(parts_saved[w], b * 16 + 16)
                    rows = parts_dram[b, w].rearrange("k (d h) t -> k d (h t)", d=D)
                    for k in range(PARTS):
                        r0 = PARTS * D * k
                        if w == 0:
                            for j in range(PARTS):
                                sp.dma_start(q_stack[r0 + D * j:r0 + D * (j + 1), b, :], rows[k]).then_inc(stack_loaded, 16)
                        else:
                            sp.dma_start(k_stack[r0:r0 + PARTS * D, b, :],
                                         rows.rearrange("k d n -> (k d) n")).then_inc(stack_loaded, 16)

            def load_shift(b):
                sp.wait_ge(shiftT_copied, b + 1)
                sp.dma_start(shift_dram[b].rearrange("(k c) q -> c k q", k=2), shiftT[:]).then_inc(shift_saved, 16)
                sp.wait_ge(shift_saved, b * 16 + 16)
                sp.dma_start(q_stack[SHIFT_ROW:ROWS, b, :], shift_dram[b].rearrange("(k c) q -> k (c q)", k=PARTS)).then_inc(shift_loaded, 16)

            def save_heads(b):
                for hg in range(NHG):
                    sp.wait_ge(heads_copied, b * NHG + hg + 1)
                    sp.dma_start(heads_dram[b, hg * P:(hg + 1) * P, :], heads_sb[:, hg % 2, :]).then_inc(heads_saved[hg % 2], 16)

            load_shift(0)
            with sp.Fori(1, NB) as b:
                save_heads(b - 1)
                load_shift(b)
            save_heads(NB - 1)

            for b in range(NB):
                for s in range(2):
                    sp.wait_ge(heads_saved[s], 16 * 2 * (b + 1))
                rows = heads_dram[b].rearrange("(h r) t -> h r t", r=AUG)
                if b == 0:
                    sp.wait_ge(pv_done, NG)
                for h in range(H):
                    sp.dma_start(numer[h * D:(h + 1) * D, b * T:(b + 1) * T], rows[h, 0:D, :]).then_inc(sums_loaded[b], 16)
                    sp.dma_start(denom[h * D:(h + 1) * D, b * T:(b + 1) * T], rows[h, D:2 * D, :]).then_inc(sums_loaded[b], 16)

            with sp.Fori(0, NT // 2) as tp:
                for s in range(2):
                    sp.wait_ge(y_ready, tp * 2 + s + 1)
                    sp.dma_start(out_tiles[:, ds(tp * 2 + s, 1), :], y_sb[:, s:s + 1, :]).then_inc(y_saved[s], 16)
            for s in range(2):
                sp.wait_ge(y_saved[s], 16 * NT // 2)

        @block.gpsimd
        def _(pool):
            nc.gpsimd.memset(v_aug[:, :, :, D:2 * D], 1.0).then_inc(aug_filled, 1)
            nc.gpsimd.memset(v_aug[:, :, :, 2 * D:AUG], 0.0).then_inc(aug_filled, 1)
            with pool.Fori(0, NB) as b:
                for w in range(2):
                    step = b * 8 + 4 * w
                    pool.wait_ge(rope_read, b * 4 + 2 * (w + 1))
                    pool.wait_ge(split_step, step)
                    nc.gpsimd.tensor_tensor(rotated[:, w], rot[:, w, 0], rot[:, w, 1], ALU.add).then_inc(split_step, 1)
                    pool.wait_ge(parts_saved[w], b * 16)
                    nc.gpsimd.tensor_tensor(parts[:, w, 0], rot[:, w, 0], rot[:, w, 1], ALU.add).then_inc(rope_added[w], 1)
                    pool.wait_ge(rope_added[w], b + 1)
                    pool.wait_ge(split_step, step + 1)
                    nc.gpsimd.tensor_tensor(rest[:, w], rotated[:, w], parts[:, w, 0], ALU.subtract).then_inc(split_step, 1)
                    nc.gpsimd.tensor_tensor(parts[:, w, 1], rotated[:, w], parts[:, w, 0], ALU.subtract).then_inc(split_step, 1)
                    pool.wait_ge(split_step, step + 3)
                    nc.gpsimd.tensor_tensor(parts[:, w, 2], rest[:, w], parts[:, w, 1], ALU.subtract).then_inc(split_step, 1)
                    pool.wait_ge(split_step, step + 4)
                    pool.sem_inc(parts_ready[w], 1)

            with pool.Fori(0, NB) as b:
                pool.wait_ge(v_copied, b + 1)
                pool.wait_ge(pv_done, b * NG)
                pool.wait_ge(aug_filled, 2)
                nc.gpsimd.tensor_copy(v_aug[:, :, :, 0:D],
                                      v_all[:, ds(b * QT, QT), :].rearrange("p t (h d) -> p t h d", h=H)).then_inc(v_aug_ready, 1)

            pool.wait_ge(rstd2_done, 1)
            pool.wait_ge(moments2_done, NT)
            for t in range(NT):
                nc.gpsimd.tensor_scalar(xn2[:, t], x_sb[:, t], moments[:, t, 0:1], rstd[:, t:t + 1],
                                        ALU.subtract, ALU.mult).then_inc(xn2_ready, 1)

            pool.wait_ge(xn2T_copied, NB)
            with pool.Fori(0, NT // 2) as tp:
                for s in range(2):
                    pool.wait_ge(up_done, tp * 16)
                    nc.gpsimd.tensor_copy(stage[:, s, :], xn2T[:, ds(tp * 2 * P + s * P, P)]).then_inc(staged[s], 1)

        @block.scalar
        def _(act):
            loads = [(w_raw[:, 0], wq), (wd_sb[:], w_down), (w_raw[0:L, 1], wk_up), (w_raw[0:L, 2], wv_up),
                     (w_raw[:, 3], wo)]
            for dst, src in loads:
                act.dma_start(dst, src).then_inc(w_loaded, 16)
            for dst, src in ((eye[:], c_eye), (eye16[:], c_eye16), (rope[:].rearrange("p k t -> p (k t)"), c_rope),
                             (expert_no[:], c_expert)):
                act.dma_start(dst, src).then_inc(c_loaded, 16)
            act.dma_start(gw_sb[:], gate_w).then_inc(g_loaded, 16)
            act.dma_start(bias_sb[:], expert_bias.unsqueeze(0).to_broadcast([P, NE])).then_inc(g_loaded, 16)

            act.wait_ge(var_done, 1)
            nc.scalar.activation(rstd[:], rstd[:], ACT.Sqrt).then_inc(std_done, 1)

            with act.Fori(0, NB) as b:
                act.wait_ge(xT_ps, b + 1)
                act.wait_ge(v_ps, b)
                nc.scalar.copy(xT[:], ps_o[:]).then_inc(xT_copied, 1)
                act.wait_ge(v_ps, b + 1)
                nc.scalar.copy(v_all[:, ds(b * QT, QT), :].rearrange("p t e -> p (t e)"), ps_a[:, 0]).then_inc(v_copied, 1)

            act.wait_ge(split_step, 8 * NB)

            def copy_heads(b, hg):
                act.wait_ge(pv_done, b * NG + QT * (hg + 1))
                act.wait_ge(heads_saved[hg % 2], b * 32 + 16 * (hg // 2))
                nc.scalar.copy(heads_sb[:, hg % 2, :], ps_o[:]).then_inc(heads_copied, 1)

            with act.Fori(0, NB) as b:
                for hg in range(NHG):
                    for kt in range(QT):
                        g = hg * QT + kt
                        n = T - P * kt
                        act.wait_ge(pv_done, b * NG + max(g - 1, 0))
                        for j in range(2):
                            act.wait_ge(scores_ready, b * NPAIR + 2 * g + j + 1)
                            nc.scalar.activation(prob[:, g % 2, 2 * j:2 * j + 2, 0:n], ps_b2[:, j, :, 0:n], ACT.Exp,
                                                 scale=SCALE).then_inc(exp_done, 1)
                        if kt == 0 and hg > 0:
                            copy_heads(b, hg - 1)
                copy_heads(b, NHG - 1)

            act.wait_ge(pv_done, 2 * NG)
            act.wait_ge(max_read, NB * NMU)
            for e in range(NE):
                act.dma_start(w13[:, e, 0, :], w1[e]).then_inc(w13_loaded, 16)
                act.dma_start(w13[:, e, 1, :], w3[e]).then_inc(w13_loaded, 16)
                for j, (j0, nj) in enumerate(HJ):
                    act.dma_start(w2_sb[0:nj, e, j, :], w2[e, j0:j0 + nj, :]).then_inc(w2_loaded, 16)

            act.wait_ge(var2_done, 1)
            nc.scalar.activation(rstd[:], rstd[:], ACT.Sqrt).then_inc(std2_done, 1)
            for b in range(NB):
                act.wait_ge(xn2T_ps, b + 1)
                nc.scalar.copy(xn2T[:, b * T:(b + 1) * T], ps_b[:, b]).then_inc(xn2T_copied, 1)
            act.wait_ge(route_step, 2)
            nc.scalar.activation(route[:, 2], route[:, 1], ACT.Exp).then_inc(gate_exp, 1)

            act.wait_ge(route_step, ROUTE_STEPS)
            with act.Fori(0, NT // 2) as tp:
                def silu(n):
                    act.wait_ge(up_done, tp * 16 + n + 1)
                    act.wait_ge(hid_done, tp * 16 + max(n - 1, 0))
                    nc.scalar.activation(gate[:, n % 2, :], ps_a[:, n % 2, 0:HID], ACT.Silu,
                                         scale=weight[:, ds(tp * 16 + n, 1)]).then_inc(gate_done, 1)

                def copyT(n):
                    act.wait_ge(hidT_ps, tp * 16 + n + 1)
                    act.wait_ge(down_done, tp * 16 + max(n - 1, 0))
                    nc.scalar.copy(hidT[:, n % 2, 0:2 * P], ps_b[:, 2 + n % 2, 0:2 * P]).then_inc(hidT_copied, 1)

                for n in range(16):
                    silu(n)
                    if n:
                        copyT(n - 1)
                copyT(15)


        @block.vector
        def _(dve):
            def norm_stats(src, stats_done, moments_done, var_done, std_done, rstd_done):
                for t in range(NT):
                    nc.vector.bn_stats(stats[:, t, :], src[:, t, :]).then_inc(stats_done, 1)
                for t in range(NT):
                    dve.wait_ge(stats_done, t + 1)
                    nc.vector.bn_aggr(moments[:, t, :], stats[:, t, :]).then_inc(moments_done, 1)
                dve.wait_ge(moments_done, NT)
                nc.vector.tensor_scalar(rstd[:], moments[:, :, 1], EPS, None, ALU.add).then_inc(var_done, 1)
                dve.wait_ge(std_done, 1)
                nc.vector.reciprocal(rstd[:], rstd[:]).then_inc(rstd_done, 1)

            for b in range(NB):
                dve.wait_ge(x_loaded[b], 16)
            norm_stats(x_sb, stats_done, moments_done, var_done, std_done, rstd_done)

            def permuted(i, src):
                v = src.rearrange("p (h i two) -> p i two h", i=D // 2, two=2)
                own = w_proj[:, i].rearrange("p (i two h) -> p i two h", i=D // 2, two=2)
                swapped = w_proj[:, i + 1].rearrange("p (i two h) -> p i two h", i=D // 2, two=2)
                for c in range(2):
                    nc.vector.tensor_copy(own[:, :, c], v[:, :, c]).then_inc(w_ready, 1)
                    nc.vector.tensor_copy(swapped[:, :, c], v[:, :, 1 - c]).then_inc(w_ready, 1)

            dve.wait_ge(w_loaded, 16 * 5)
            permuted(0, w_raw[:, 0])
            dve.wait_ge(wdT_ps, 1)
            nc.vector.tensor_copy(wdT[:], ps_m[0:L, 0:E]).then_inc(wdT_done, 1)
            dve.wait_ge(wkv_ps, 1)
            permuted(2, ps_m[:, 0:E])
            nc.vector.tensor_copy(w_proj[:, 4], ps_m[:, E:2 * E]).then_inc(w_ready, 1)

            dve.wait_ge(c_loaded, 16 * 4)
            def rotate(b, w):
                dve.wait_ge(rope_added[w], b)
                for c in range(2):
                    dve.wait_ge(proj_done, b * 4 + 2 * w + c + 1)
                    nc.vector.tensor_tensor(rot[:, w, c], ps_b[:, 2 * w + c], rope[:, c], ALU.mult).then_inc(rope_read, 1)

            def normalise(b):
                dve.wait_ge(xT_ps, b)
                for j in range(QT):
                    t = b * QT + j
                    nc.vector.tensor_scalar(xn[:, j], x_sb[:, ds(t, 1), :].rearrange("p a e -> p (a e)"),
                                            moments[:, ds(t, 1), 0], rstd[:, ds(t, 1)],
                                            ALU.subtract, ALU.mult).then_inc(xn_ready, 1)

            dve.wait_ge(rstd_done, 1)
            normalise(0)
            with dve.Fori(0, NB - 1) as b:
                rotate(b, 0)
                normalise(b + 1)
                rotate(b, 1)
            rotate(NB - 1, 0)
            rotate(NB - 1, 1)

            with dve.Fori(0, NB) as b:
                dve.wait_ge(shift_step, b * 4)
                m3 = negmax[:, :].rearrange("p (h q) -> p q h", q=QT)
                for n, (qt, h, nh) in enumerate(MAX_UNITS):
                    keys = P * (qt + 1)
                    dve.wait_ge(max_scores, b * NMU + n + 1)
                    nc.vector.tensor_reduce(m3[:, qt, h:h + nh],
                                            ps_a[:, n % 2, 0:nh * keys].rearrange("p (a k) -> p a k", a=nh),
                                            AXX, ALU.max, negate=True).then_inc(max_read, 1)
                dve.wait_ge(max_read, b * NMU + NMU)
                dve.wait_ge(shiftT_done, b)
                nc.vector.tensor_copy(shift[:, 0], negmax[:]).then_inc(shift_step, 1)
                dve.wait_ge(shift_step, b * 4 + 1)
                nc.vector.tensor_tensor(shift_rest[:], negmax[:], shift[:, 0], ALU.subtract).then_inc(shift_step, 1)
                dve.wait_ge(shift_step, b * 4 + 2)
                nc.vector.tensor_copy(shift[:, 1], shift_rest[:]).then_inc(shift_step, 1)
                dve.wait_ge(shift_step, b * 4 + 3)
                nc.vector.tensor_tensor(shift[:, 2], shift_rest[:], shift[:, 1], ALU.subtract).then_inc(shift_step, 1)
                dve.wait_ge(shiftT_done, b + 1)
                dve.wait_ge(shift_saved, b * 16)
                nc.vector.tensor_copy(shiftT[:], shiftT_ps).then_inc(shiftT_copied, 1)

            for b in range(NB):
                cols = slice(b * T, (b + 1) * T)
                dve.wait_ge(sums_loaded[b], 16 * 2 * H)
                nc.vector.reciprocal(denom[:, cols], denom[:, cols]).then_inc(inv_done, 1)
                dve.wait_ge(inv_done, b + 1)
                nc.vector.tensor_tensor(numer[:, cols], numer[:, cols], denom[:, cols], ALU.mult).then_inc(normed, 1)
            for b in range(NB):
                xb = x_sb[:, QT * b:QT * (b + 1), :].rearrange("p t e -> p (t e)")
                dve.wait_ge(wo_done, b + 1)
                nc.vector.tensor_tensor(xb, ps_b[:, b], xb, ALU.add).then_inc(x2_ready, 1)
            dve.wait_ge(x2_ready, NB)
            norm_stats(x_sb, stats2_done, moments2_done, var2_done, std2_done, rstd2_done)

            dve.wait_ge(gwT_ps, 1)
            nc.vector.tensor_copy(gwT[:], ps_m[:, 0:NE]).then_inc(gwT_done, 1)

            step = [0]

            def routed(instruction):
                step[0] += 1
                instruction.then_inc(route_step, 1)
                dve.wait_ge(route_step, step[0])

            logits = ps_a[:, 0, 0:NT * NE].rearrange("p (t e) -> p t e", e=NE)
            probs, biased, top, chosen = route[:, 3], route[:, 4], route[:, 5], route[:, 6]
            number = route[:, 7]
            col = route[:, 0, :, 0:1]
            over = lambda a: a.to_broadcast([P, NT, NE])
            dve.wait_ge(logits_done, 1)
            routed(nc.vector.tensor_reduce(route[:, 0, :, 0], logits, AXX, ALU.max))
            routed(nc.vector.tensor_tensor(route[:, 1], logits, over(col), ALU.subtract))
            dve.wait_ge(gate_exp, 1)
            routed(nc.vector.tensor_reduce(route[:, 0, :, 1], route[:, 2], AXX, ALU.add))
            routed(nc.vector.reciprocal(route[:, 0, :, 2], route[:, 0, :, 1]))
            routed(nc.vector.tensor_tensor(probs, route[:, 2], over(route[:, 0, :, 2:3]), ALU.mult))
            routed(nc.vector.tensor_tensor(biased, probs, bias_sb[:].unsqueeze(1).to_broadcast([P, NT, NE]), ALU.add))
            for t in range(NT):
                routed(nc.vector.max(top[:, t], biased[:, t]))
            for t in range(NT):
                routed(nc.vector.max_index(chosen[:, t].bitcast(U32), top[:, t], biased[:, t]))
            routed(nc.vector.tensor_copy(number, chosen.bitcast(U32)))
            for k in range(2):
                routed(nc.vector.tensor_tensor(route[:, 8 + k], expert_no[:].unsqueeze(1).to_broadcast([P, NT, NE]),
                                               over(number[:, :, k:k + 1]), ALU.is_equal))
            routed(nc.vector.tensor_tensor(route[:, 10], route[:, 8], route[:, 9], ALU.add))
            routed(nc.vector.tensor_tensor(route[:, 11], route[:, 10], probs, ALU.mult))
            assert step[0] == ROUTE_STEPS, step[0]

            with dve.Fori(0, NT // 2) as tp:
                def product(n):
                    dve.wait_ge(gate_done, tp * 16 + n + 1)
                    dve.wait_ge(hidT_ps, tp * 16 + max(n - 1, 0))
                    nc.vector.scalar_tensor_tensor(hid[:, n % 2, :], ps_b[:, n % 2, 0:HID],
                                                   weight[:, ds(tp * 16 + n, 1)], gate[:, n % 2, :],
                                                   ALU.mult, ALU.mult).then_inc(hid_done, 1)

                def copyT(n):
                    dve.wait_ge(hidT_copied, tp * 16 + n + 1)
                    dve.wait_ge(down_done, tp * 16 + max(n - 1, 0))
                    nc.vector.tensor_copy(hidT[0:HJ[2][1], n % 2, 2 * P:3 * P], ps_b[0:HJ[2][1], 2 + n % 2, 2 * P:3 * P]).then_inc(hidT_copied2, 1)

                def result(s):
                    dve.wait_ge(down_done, tp * 16 + 8 * (s + 1))
                    dve.wait_ge(y_saved[s], tp * 16)
                    bank = (ps_o, ps_m)[s]
                    nc.vector.tensor_tensor(y_sb[:, s, :], bank[:, 0:E], x_sb[:, ds(tp * 2 + s, 1), :].rearrange("p a e -> p (a e)"),
                                            ALU.add).then_inc(y_ready, 1)

                for n in range(16):
                    product(n)
                    if n:
                        copyT(n - 1)
                    if n == 10:
                        result(0)
                copyT(15)
                result(1)

        @block.tensor
        def _(pe):
            pe.wait_ge(w_loaded, 16 * 5)
            pe.wait_ge(c_loaded, 16 * 4)
            nc.tensor.transpose(ps_m[0:L, 0:E], wd_sb[:], eye[:]).then_inc(wdT_ps, 1)
            pe.wait_ge(wdT_done, 1)
            nc.tensor.matmul(ps_m[:, 0:E], wdT[:], w_raw[0:L, 1], start=True, stop=True)
            nc.tensor.matmul(ps_m[:, E:2 * E], wdT[:], w_raw[0:L, 2], start=True, stop=True).then_inc(wkv_ps, 1)
            pe.wait_ge(w_ready, 9)

            with pe.Fori(0, NB) as b:
                pe.wait_ge(xn_ready, b * QT + QT)
                pe.wait_ge(xT_copied, b)
                for j in range(QT):
                    last = nc.tensor.transpose(ps_o[:, j * P:(j + 1) * P], xn[:, j, :], eye[:])
                last.then_inc(xT_ps, 1)
                pe.wait_ge(xT_copied, b + 1)
                pe.wait_ge(rope_read, b * 4)
                for i in range(4):
                    nc.tensor.matmul(ps_b[:, i], w_proj[:, i], xT[:], start=True, stop=True).then_inc(proj_done, 1)
                pe.wait_ge(v_copied, b)
                for j in range(QT):
                    last = nc.tensor.matmul(ps_a[:, 0, j * P:(j + 1) * P], xT[:, j * P:(j + 1) * P], w_proj[:, 4], start=True, stop=True)
                last.then_inc(v_ps, 1)

            def qs(b, h, t0, n, rows):
                return q_stack[0:rows, b, h * T + t0:h * T + t0 + n]

            def ks(b, h, t0, n, rows):
                return k_stack[0:rows, b, h * T + t0:h * T + t0 + n]

            def max_unit(b, n):
                qt, h0, nh = MAX_UNITS[n]
                keys = P * (qt + 1)
                if n == 0:
                    pe.wait_ge(stack_loaded, b * STACK_DMAS + STACK_DMAS)
                if n >= 2:
                    pe.wait_ge(max_read, b * NMU + n - 1)
                elif n == 0:
                    pe.wait_ge(max_read, b * NMU)
                for a in range(nh):
                    last = nc.tensor.matmul(ps_a[:, n % 2, a * keys:(a + 1) * keys], qs(b, h0 + a, qt * P, P, SHIFT_ROW),
                                            ks(b, h0 + a, 0, keys, SHIFT_ROW), start=True, stop=True)
                last.then_inc(max_scores, 1)

            def transpose_shift(b):
                pe.wait_ge(shift_step, b * 4 + 4)
                pe.wait_ge(shiftT_copied, b)
                for k in range(2):
                    last = nc.tensor.transpose(shiftT_ps[:, k, :], shift_cols[:, k * SR:(k + 1) * SR], eye16[:])
                last.then_inc(shiftT_done, 1)

            def scores(b, g, j):
                hg, kt = divmod(g, QT)
                if g == 0 and j == 0:
                    pe.wait_ge(shift_loaded, b * 16 + 16)
                u = 2 * g + j
                pe.wait_ge(exp_done, b * NPAIR + max(u - 1, 0))
                for a in range(2):
                    h = HG * hg + 2 * j + a
                    last = nc.tensor.matmul(ps_b2[:, j, a, 0:T - kt * P], ks(b, h, kt * P, P, ROWS),
                                            qs(b, h, kt * P, T - kt * P, ROWS), start=True, stop=True)
                last.then_inc(scores_ready, 1)

            def values(b, g):
                hg, kt = divmod(g, QT)
                pe.wait_ge(exp_done, b * NPAIR + 2 * g + 2)
                if g == 0:
                    pe.wait_ge(v_aug_ready, b + 1)
                if kt == 0:
                    pe.wait_ge(heads_copied, b * NHG + hg)
                for a in range(HG):
                    last = nc.tensor.matmul(ps_o[a * AUG:(a + 1) * AUG, kt * P:T], v_aug[:, kt, HG * hg + a, :],
                                            prob[:, g % 2, a, 0:T - kt * P], start=kt == 0, stop=kt == QT - 1)
                last.then_inc(pv_done, 1)

            pe.wait_ge(rows_loaded, 16 * 2 * NB)
            pe.wait_ge(rope_read, 4 * NB)
            pe.wait_ge(v_copied, NB)
            for n in range(NMU):
                max_unit(0, n)
            transpose_shift(0)
            with pe.Fori(1, NB) as b:
                n = 0
                for g in range(NG):
                    want = min(NMU, 6 + (NMU - 6) * g // (NG - 1))
                    for j in range(2):
                        mid = want if j else (n + want) // 2
                        while n < mid:
                            max_unit(b, n)
                            n += 1
                        scores(b - 1, g, j)
                    if g:
                        values(b - 1, g - 1)
                values(b - 1, NG - 1)
                transpose_shift(b)
            for g in range(NG):
                for j in range(2):
                    scores(NB - 1, g, j)
                if g:
                    values(NB - 1, g - 1)
            values(NB - 1, NG - 1)

            pe.wait_ge(exp_done, NB * NPAIR)
            for b in range(NB):
                pe.wait_ge(normed, b + 1)
                for j in range(QT):
                    last = nc.tensor.matmul(ps_b[:, b, j * P:(j + 1) * P], numer[:, (b * QT + j) * P:(b * QT + j + 1) * P],
                                            w_raw[:, 3], start=True, stop=True)
                last.then_inc(wo_done, 1)
            pe.wait_ge(g_loaded, 32)
            pe.wait_ge(shiftT_copied, NB)
            nc.tensor.transpose(ps_m[:, 0:NE], gw_sb[:], eye[0:NE, 0:NE]).then_inc(gwT_ps, 1)

            pe.wait_ge(x2_ready, NB)
            for b in range(NB):
                pe.wait_ge(xn2_ready, QT * (b + 1))
                for j in range(QT):
                    last = nc.tensor.transpose(ps_b[:, b, j * P:(j + 1) * P], xn2[:, b * QT + j, :], eye[:])
                last.then_inc(xn2T_ps, 1)
            pe.wait_ge(gwT_done, 1)
            pe.wait_ge(max_read, NB * NMU)
            for t in range(NT):
                if t % QT == 0:
                    pe.wait_ge(xn2T_copied, t // QT + 1)
                last = nc.tensor.matmul(ps_a[:, 0, t * NE:(t + 1) * NE], xn2T[:, t * P:(t + 1) * P], gwT[:], start=True, stop=True)
            last.then_inc(logits_done, 1)

            pe.wait_ge(w13_loaded, 16 * 2 * NE)
            pe.wait_ge(w2_loaded, 16 * 3 * NE)
            pe.wait_ge(route_step, 2)
            pe.wait_ge(heads_copied, NB * NHG)
            with pe.Fori(0, NT // 2) as tp:
                def up(n):
                    s, e = divmod(n, NE)
                    if e == 0:
                        pe.wait_ge(staged[s], tp + 1)
                    pe.wait_ge(gate_done, tp * 16 + max(n - 1, 0))
                    pe.wait_ge(hid_done, tp * 16 + max(n - 1, 0))
                    nc.tensor.matmul(ps_a[:, n % 2, 0:HID], stage[:, s, :], w13[:, e, 0, :], start=True, stop=True)
                    nc.tensor.matmul(ps_b[:, n % 2, 0:HID], stage[:, s, :], w13[:, e, 1, :], start=True, stop=True).then_inc(up_done, 1)

                def turn(n):
                    pe.wait_ge(hid_done, tp * 16 + n + 1)
                    pe.wait_ge(hidT_copied, tp * 16 + max(n - 1, 0))
                    pe.wait_ge(hidT_copied2, tp * 16 + max(n - 1, 0))
                    for j, (j0, nj) in enumerate(HJ):
                        last = nc.tensor.transpose(ps_b[0:nj, 2 + n % 2, j * P:(j + 1) * P], hid[:, n % 2, j0:j0 + nj], eye[:])
                    last.then_inc(hidT_ps, 1)

                def down(n):
                    s, e = divmod(n, NE)
                    if e == 0:
                        pe.wait_ge(y_ready, tp * 2)
                    pe.wait_ge(hidT_copied, tp * 16 + n + 1)
                    pe.wait_ge(hidT_copied2, tp * 16 + n + 1)
                    bank = (ps_o, ps_m)[s]
                    for j, (j0, nj) in enumerate(HJ):
                        last = nc.tensor.matmul(bank[:, 0:E], hidT[0:nj, n % 2, j * P:(j + 1) * P], w2_sb[0:nj, e, j, :],
                                                start=(e == 0 and j == 0), stop=(e == NE - 1 and j == 2))
                    last.then_inc(down_done, 1)

                for n in range(18):
                    if n < 16:
                        up(n)
                    if 1 <= n < 17:
                        turn(n - 1)
                    if n >= 2:
                        down(n - 2)


ROUTE_STEPS = 11 + 2 * NT
STACK_DMAS = 16 * (PARTS * PARTS + PARTS)

_INS = ["L0_attn_x", "L0_attn_wq", "L0_attn_w_down", "L0_attn_wk_up", "L0_attn_wv_up", "L0_attn_wo",
        "L0_ffn_gate_w", "L0_ffn_expert_bias", "L0_ffn_w1", "L0_ffn_w2", "L0_ffn_w3"]


def kernel(**inputs):
    import concourse.bacc as bacc
    from concourse.bass_utils import run_bass_kernel_spmd

    nc = bacc.Bacc("TRN2", target_bir_lowering=False, num_devices=1)
    arrays, args = {}, []
    for name in _INS:
        a = np.ascontiguousarray(inputs[name])
        arrays[name] = a
        args.append(nc.dram_tensor(name, a.shape, mybir.dt.from_np(a.dtype), kind="ExternalInput").ap())
    out = nc.dram_tensor("out", (NB, T, E), F32, kind="ExternalOutput").ap()
    consts = {}
    for name, a in constants().items():
        arrays[name] = a
        consts[name] = nc.dram_tensor(name, a.shape, mybir.dt.from_np(a.dtype), kind="ExternalInput").ap()
    build_block(nc, *args, out, **consts)
    r = run_bass_kernel_spmd(nc, [arrays], core_ids=[0])
    return r.results[0]["out"]
```

```python
from contextlib import ExitStack

import numpy as np

import concourse.bass as bass
from concourse import mybir

F32 = mybir.dt.float32
BF16 = mybir.dt.bfloat16
U32 = mybir.dt.uint32
I32 = mybir.dt.int32
ALU = mybir.AluOpType
ACT = mybir.ActivationFunctionType
AXX = mybir.AxisListType.X

P = 128
NB, T, E = 4, 512, 128
H = 16
D = E // H
L = E // 2
PAGE = 32
NPAGE = T // PAGE
QT = T // P
NT = NB * QT
EPS = 1e-5
SCALE = 1.0 / float(np.sqrt(D))

PARTS = 3
MASK_ROW = PARTS * PARTS * D
SHIFT_ROW = MASK_ROW + NPAGE
ROWS = SHIFT_ROW + PARTS
BIG = 2.0 ** 126

SR = PARTS * H * QT // 2

HG = 4
NHG = H // HG
AUG = 32

NE, HID = 8, 352
HJ = [(0, 128), (128, 128), (256, 96)]

REGION = NB * T + P
NBLK = -(-(2 * NB * T + NE * (P - 1)) // P)
NBLK += -NBLK % 4
ROW = E + 1
NOWHERE = 1 << 20

MAX_UNITS = ([(3, h, 1) for h in range(H)] + [(2, h, 1) for h in range(H)]
             + [(1, h, 2) for h in range(0, H, 2)] + [(0, h, 4) for h in range(0, H, 4)])
NMU = len(MAX_UNITS)
NG = NHG * QT
NPAIR = 2 * NG


def constants():
    bf = mybir.dt.np(BF16)
    inv = 1.0 / 10000.0 ** (np.arange(0, D, 2, dtype=np.float32) / D)
    ang = np.outer(np.arange(T, dtype=np.float32), inv)
    cos, sin = np.cos(ang).astype(np.float32).T, np.sin(ang).astype(np.float32).T
    rope = np.empty((D, H, 2, T), np.float32)
    for d in range(D):
        rope[d, :, 0] = cos[d // 2]
        rope[d, :, 1] = sin[d // 2] if d % 2 else -sin[d // 2]
    page = np.arange(T) // PAGE
    rows = np.arange(NPAGE)[:, None]
    k_rows = np.concatenate([(page[None] == rows), np.ones((PARTS, T))]).astype(np.float32)
    q_rows = np.where(page[None] < rows, -BIG, 0.0).astype(np.float32)
    pad = np.zeros((P, ROW), np.float32)
    pad.view(np.int32)[:, E] = NOWHERE
    return {
        "c_rope": rope.reshape(P, 2 * T),
        "c_krows": k_rows.astype(bf),
        "c_qrows": q_rows.astype(bf),
        "c_eye": np.eye(P, dtype=np.float32),
        "c_eye16": np.eye(P).astype(bf),
        "c_count": np.stack([np.triu(np.ones((P, P)), 1), np.ones((P, P))], 1).astype(bf),
        "c_expert": np.tile(np.stack([np.arange(NE), REGION * np.arange(NE)]).astype(np.float32), (P, 1, 1)),
        "c_table": np.concatenate([
            np.repeat(np.arange(NBLK), NE), np.tril(np.ones((NE, NE))).ravel(), REGION * np.arange(NE),
            np.arange(NBLK)]).astype(np.float32)[None],
        "c_dest": (np.arange(2)[None, None] * NB * T + np.arange(NT)[None, :, None] * P
                   + np.arange(P)[:, None, None]).astype(np.int32),
        "c_pad": pad,
    }


def build_block(nc, x, wq, w_down, wk_up, wv_up, wo, gate_w, expert_bias, w1, w2, w3, out,
                c_rope, c_krows, c_qrows, c_eye, c_eye16, c_count, c_expert, c_table, c_dest, c_pad):
    ds = bass.ds
    with ExitStack() as ctx:
        def sb(name, shape, dt=F32):
            return ctx.enter_context(nc.sbuf_tensor(name, shape, dt))

        def ps(name, shape, dt=F32):
            return ctx.enter_context(nc.psum_tensor(name, shape, dt))

        def sem(name):
            return ctx.enter_context(nc.semaphore(name))

        parts_dram = nc.dram_tensor("parts_dram", (NB, 2, PARTS, P, T), BF16, kind="Internal").ap()
        shift_dram = nc.dram_tensor("shift_dram", (NB, PARTS * H * QT, P), BF16, kind="Internal").ap()
        heads_dram = nc.dram_tensor("heads_dram", (NB, NHG * P, T), F32, kind="Internal").ap()
        rows_dram = nc.dram_tensor("rows_dram", ((NE + 1) * REGION, ROW), F32, kind="Internal").ap()
        y_dram = nc.dram_tensor("y_dram", (2 * NB * T, E), F32, kind="Internal").ap()

        stack = sb("stack", [P, 2, NB, H * T], BF16)
        q_stack, k_stack = stack[:, 0], stack[:, 1]
        x_sb = sb("x_sb", [P, NT, E])
        numer = sb("numer", [P, NB * T])
        v_all = sb("v_all", [P, NT, E])
        v_aug = sb("v_aug", [P, QT, H, AUG])
        work = sb("work", [P, 8 * T])
        rope = sb("rope", [P, 2, T])
        parts = sb("parts", [P, 2, PARTS, T], BF16)
        xT = sb("xT", [P, T])
        heads_sb = sb("heads_sb", [P, 2, T])
        w_raw = sb("w_raw", [P, 4, E])
        wd_sb = sb("wd_sb", [P, L])
        wdT = sb("wdT", [L, E])
        w_proj = sb("w_proj", [P, 5, E])
        eye = sb("eye", [P, P])
        eye16 = sb("eye16", [P, P], BF16)
        count = sb("count", [P, 2, P], BF16)
        half = sb("half", [P, QT])
        stats = sb("stats", [P, QT, 6])
        moments = sb("moments", [P, NT, 2])
        veps = sb("veps", [P, NT])
        rstd = sb("rstd", [P, NT])
        negmax = sb("negmax", [P, H * QT])
        shift_rest = sb("shift_rest", [P, H * QT])
        shift = sb("shift", [P, PARTS, H * QT], BF16)
        shiftT = sb("shiftT", [SR, 2, P], BF16)
        gw_sb = sb("gw_sb", [NE, E])
        gwT = sb("gwT", [P, NE])
        bias_sb = sb("bias_sb", [P, NE])
        expert = sb("expert", [P, 2, NE])
        dest = sb("dest", [P, NT, 2], I32)
        table_in = sb("table_in", [1, NBLK * NE + NE * NE + NE + NBLK])
        free_row = sb("free_row", [1, NE], I32)
        block_table = sb("block_table", [1, 2, NBLK], I32)
        route = sb("route", [P, 12, QT * NE])
        taken = sb("taken", [P, QT * NE], BF16)
        picked = sb("picked", [P, 4, 2, QT])
        place = sb("place", [P, 2, QT], U32)

        rot = work[:, 0:4 * T].rearrange("p (w k t) -> p w k t", w=2, k=2)
        rotated = work[:, 4 * T:6 * T].rearrange("p (w t) -> p w t", w=2)
        rest = work[:, 6 * T:8 * T].rearrange("p (w t) -> p w t", w=2)
        prob = work[:, :].rearrange("p (s g t) -> p s g t", s=2, g=HG)
        tables = work[0:1, 0:2 * NBLK * NE].rearrange("p (k n) -> p k n", k=2)
        short = work[0:1, 2 * NBLK * NE:(2 * NE + 8) * NBLK].rearrange("p (k n) -> p k n", k=8)
        cut = [0]

        def of_work(*dims):
            a = cut[0]
            cut[0] += int(np.prod(dims))
            assert cut[0] <= 8 * T
            v = work[:, a:cut[0]]
            return v.rearrange("p (s n) -> p s n", s=dims[0])

        blk = of_work(4, ROW)
        blkT = of_work(2, P)
        gate = of_work(2, HID)
        hid = of_work(2, HID)
        hidT = of_work(2, 3 * P)
        y_rows = of_work(4, E)
        where = of_work(4, 1).bitcast(U32)
        xn = numer[:, 0:QT * E].rearrange("p (t e) -> p t e", e=E)
        xn2 = rope[:, 0, :].rearrange("p (t e) -> p t e", e=E)
        xn2T = rope[:, 1, :]
        rows = parts[:, :, :, :].rearrange("p w k t -> p (w k t)").bitcast(F32)[:, 0:2 * QT * ROW].rearrange(
            "p (k t n) -> p k t n", k=2, t=QT)
        area = stack[:, :, :, :].rearrange("p w b n -> p (w b n)").bitcast(F32)
        SEQ = H * T // 2
        denom = area[:, 0:NB * T]
        w13 = area[:, NB * T:NB * T + NE * 2 * HID].rearrange("p (e w n) -> p e w n", e=NE, w=2)
        assert NB * T + NE * 2 * HID <= 2 * SEQ
        k_area = area[:, NB * SEQ:]
        w2_sb = k_area[:, 0:NE * 3 * E].rearrange("p (e j n) -> p e j n", e=NE, j=3)
        y_sb = k_area[:, SEQ:2 * SEQ].rearrange("p (k t e) -> p k t e", k=2, e=E)
        assert NE * 3 * E <= SEQ and 2 * NT * E <= SEQ

        ps_a = ps("ps_a", [P, 2, T])
        ps_b = ps("ps_b", [P, 4, T])
        ps_o = ps("ps_o", [P, T])
        ps_m = ps("ps_m", [P, T])
        ps_b2 = ps_b[:, :, :].rearrange("p (s w) t -> p s w t", s=2)
        shiftT_ps = ps_m[0:SR, 0:P].bitcast(BF16).rearrange("p (k q) -> p k q", k=2)
        shift_cols = shift[:, :, :].rearrange("p k c -> p (k c)")

        GRANT, GRANT_DMA = 1, 16
        x_loaded = [sem(f"x_loaded{b}") for b in range(NB)]
        w_loaded, c_loaded, r_loaded = sem("w_loaded"), sem("c_loaded"), sem("r_loaded")
        rows_loaded = sem("rows_loaded")
        stats_done, moments_done, var_done = sem("stats_done"), sem("moments_done"), sem("var_done")
        half_set, rstd_done, xn_ready = sem("half_set"), sem("rstd_done"), sem("xn_ready")
        wdT_ps, wdT_done, wkv_ps, w_ready = sem("wdT_ps"), sem("wdT_done"), sem("wkv_ps"), sem("w_ready")
        xT_ps, xT_copied = sem("xT_ps"), sem("xT_copied")
        proj_done, rope_read = sem("proj_done"), sem("rope_read")
        v_ps, v_copied = sem("v_ps"), sem("v_copied")
        sum_done, part0_done, rest_done, part1_done = sem("sum_done"), sem("part0_done"), sem("rest_done"), sem("part1_done")
        parts_ready = sem("parts_ready")
        parts_saved = [sem("q_parts_saved"), sem("k_parts_saved")]
        stack_loaded = [sem(f"stack_loaded{b}") for b in range(NB)]
        max_scores, max_read = sem("max_scores"), sem("max_read")
        shift_step = sem("shift_step")
        shiftT_done, shiftT_copied = sem("shiftT_done"), sem("shiftT_copied")
        shift_saved, shift_loaded = sem("shift_saved"), sem("shift_loaded")
        aug_filled, v_aug_ready = sem("aug_filled"), sem("v_aug_ready")
        scores_ready, exp_done, pv_done = sem("scores_ready"), sem("exp_done"), sem("pv_done")
        heads_copied = sem("heads_copied")
        heads_saved = [sem("heads_saved0"), sem("heads_saved1")]
        sums_loaded = sem("sums_loaded")
        experts_loaded, pad_saved = sem("experts_loaded"), sem("pad_saved")
        gwT_ps, gwT_done = sem("gwT_ps"), sem("gwT_done")
        inv_done, normed, wo_done, x2_ready = sem("inv_done"), sem("normed"), sem("wo_done"), sem("x2_ready")
        stats2, moments2, var2, rstd2 = sem("stats2"), sem("moments2"), sem("var2"), sem("rstd2")
        xn2_ready, xn2T_ps, xn2T_copied = sem("xn2_ready"), sem("xn2T_ps"), sem("xn2T_copied")
        logits_done, route_step, gate_in, gate_exp = sem("logits_done"), sem("route_step"), sem("gate_in"), sem("gate_exp")
        taken_ready, ranked, rows_ready, place_ready = sem("taken_ready"), sem("ranked"), sem("rows_ready"), sem("place_ready")
        go_rows, rows_sent, rows_free = sem("go_rows"), sem("rows_sent"), sem("rows_free")
        best_found, go_next = sem("best_found"), sem("go_next")
        table_step, table_ready = sem("table_step"), sem("table_ready")
        blk_loaded = [sem(f"blk_loaded{k}") for k in range(4)]
        where_done, blkT_ps, blkT_copied = sem("where_done"), sem("blkT_ps"), sem("blkT_copied")
        up_done, gate_done, hid_done = sem("up_done"), sem("gate_done"), sem("hid_done")
        hidT_ps, hidT_copied, down_done, y_ready = sem("hidT_ps"), sem("hidT_copied"), sem("down_done"), sem("y_ready")
        go_load, go_scatter = sem("go_load"), sem("go_scatter")
        y_sent = [sem(f"y_sent{k}") for k in range(4)]
        y_loaded = [sem(f"y_loaded{b}") for b in range(NB)]
        y_added, out_ready, out_saved = sem("y_added"), sem("out_ready"), sem("out_saved")

        block = ctx.enter_context(nc.Block())

        x_tiles = x.rearrange("b (t p) e -> p (b t) e", p=P)
        out_tiles = out.rearrange("b (t p) e -> p (b t) e", p=P)

        def tiles(b):
            return slice(QT * b, QT * (b + 1))

        @block.sync
        def _(sp):
            sp.sem_inc(shift_saved, GRANT_DMA)
            for s in range(2):
                sp.sem_inc(heads_saved[s], GRANT_DMA)
            for b in range(NB):
                sp.dma_start(x_sb[:, tiles(b), :], x_tiles[:, tiles(b), :]).then_inc(x_loaded[b], 16)
                if b == 0:
                    sp.dma_start(wd_sb[:], w_down).then_inc(w_loaded, 16)
            for b in range(NB):
                sp.dma_start(q_stack[MASK_ROW:SHIFT_ROW, b, :].rearrange("p (h t) -> p h t", h=H),
                             c_qrows.unsqueeze(1).to_broadcast([NPAGE, H, T])).then_inc(rows_loaded, 16)
                sp.dma_start(k_stack[MASK_ROW:ROWS, b, :].rearrange("p (h t) -> p h t", h=H),
                             c_krows.unsqueeze(1).to_broadcast([NPAGE + PARTS, H, T])).then_inc(rows_loaded, 16)

            for b in range(NB):
                for w in range(2):
                    sp.wait_ge(parts_ready, 2 * b + w + 1)
                    sp.dma_start(parts_dram[b, w].rearrange("k p t -> p k t"), parts[:, w]).then_inc(parts_saved[w], 16)
                    sp.wait_ge(parts_saved[w], 16 * (b + 1))
                    part = parts_dram[b, w].rearrange("k (d h) t -> k d (h t)", d=D)
                    for k in range(PARTS):
                        r0 = PARTS * D * k
                        if w == 0:
                            sp.dma_start(q_stack[r0:r0 + PARTS * D, b, :],
                                         part[k:k + 1].to_broadcast([PARTS, D, H * T])).then_inc(stack_loaded[b], 16)
                        else:
                            sp.dma_start(k_stack[r0:r0 + PARTS * D, b, :],
                                         part.rearrange("k d n -> (k d) n")).then_inc(stack_loaded[b], 16)
            sp.dma_start(rows_dram[NE * REGION:NE * REGION + P, :], c_pad).then_inc(pad_saved, 16)

            def load_shift(b):
                sp.wait_ge(shiftT_copied, b + 1)
                sp.dma_start(shift_dram[b].rearrange("(k c) q -> c k q", k=2), shiftT[:]).then_inc(shift_saved, 16)
                sp.wait_ge(shift_saved, b * 16 + 16 + GRANT_DMA)
                sp.dma_start(q_stack[SHIFT_ROW:ROWS, b, :], shift_dram[b].rearrange("(k c) q -> k (c q)", k=PARTS)).then_inc(shift_loaded, 16)

            def save_heads(b):
                for hg in range(NHG):
                    sp.wait_ge(heads_copied, b * NHG + hg + 1 + GRANT)
                    sp.dma_start(heads_dram[b, hg * P:(hg + 1) * P, :], heads_sb[:, hg % 2, :]).then_inc(heads_saved[hg % 2], 16)

            def load_sums(b):
                for s in range(2):
                    sp.wait_ge(heads_saved[s], b * 32 + 32 + GRANT_DMA)
                head = heads_dram[b].rearrange("(h r) t -> h r t", r=AUG)
                sp.dma_start(numer[:, ds(b * T, T)], head[:, 0:D, :]).then_inc(sums_loaded, 16)
                sp.dma_start(denom[:, ds(b * T, T)], head[:, D:2 * D, :]).then_inc(sums_loaded, 16)
                sp.wait_ge(sums_loaded, b * 32 + 32)

            load_shift(0)
            with sp.Fori(1, NB) as b:
                save_heads(b - 1)
                load_shift(b)
                load_sums(b - 1)
                sp.sem_inc(go_load, 1)
            sp.wait_ge(pv_done, 2 * NG + GRANT)
            sp.wait_ge(max_read, NB * NMU)
            sp.dma_start(w13[:, :, 0, :], w1.rearrange("e k n -> k e n")).then_inc(experts_loaded, 16)
            sp.dma_start(w13[:, :, 1, :], w3.rearrange("e k n -> k e n")).then_inc(experts_loaded, 16)
            for j, (j0, nj) in enumerate(HJ):
                sp.dma_start(w2_sb[0:nj, :, j, :], w2[:, j0:j0 + nj, :].rearrange("e k n -> k e n")).then_inc(experts_loaded, 16)
            save_heads(NB - 1)
            load_sums(NB - 1)

            sp.wait_ge(table_ready, 1)
            for e in range(NE):
                row = sp.value_load(free_row[0:1, e:e + 1], min_val=e * REGION, max_val=(e + 1) * REGION - P)
                sp.dma_start(rows_dram[ds(row, P), :], c_pad).then_inc(pad_saved, 16)

            def load_block(n, k):
                row = sp.value_load(block_table[0:1, 0, ds(n, 1)], min_val=0, max_val=NE * REGION)
                sp.dma_start(blk[:, k, :], rows_dram[ds(row, P), :]).then_inc(blk_loaded[k], 16)

            sp.wait_ge(table_ready, 2)
            sp.wait_ge(rows_sent, 16 * 2 * NT)
            sp.wait_ge(pad_saved, 16 * (NE + 1))
            for n in range(4):
                load_block(n, n)
            with sp.Fori(1, NBLK // 4) as p:
                for k in range(4):
                    sp.wait_ge(blkT_ps, p * 4 + k - 3)
                    sp.wait_ge(where_done, p * 4 + k - 3)
                    sp.sem_inc(go_load, 1)
                    load_block(p * 4 + k, k)

            for k in range(4):
                sp.wait_ge(y_sent[k], 16 * (NBLK // 4))
            y_tok = y_dram.rearrange("(k t p) e -> k p t e", k=2, p=P)
            for b in range(NB):
                for k in range(2):
                    sp.dma_start(y_sb[:, k, tiles(b), :], y_tok[k, :, tiles(b), :]).then_inc(y_loaded[b], 16)
            for b in range(NB):
                sp.wait_ge(out_ready, b + 1)
                sp.dma_start(out_tiles[:, tiles(b), :], x_sb[:, tiles(b), :]).then_inc(out_saved, 16)
            sp.wait_ge(out_saved, 16 * NB)

        @block.gpsimd
        def _(pool):
            pool.sem_inc(rows_free, GRANT)
            nc.gpsimd.memset(half[:], -0.5).then_inc(half_set, 1)
            nc.gpsimd.memset(v_aug[:, :, :, D:2 * D], 1.0).then_inc(aug_filled, 1)
            nc.gpsimd.memset(v_aug[:, :, :, 2 * D:AUG], 0.0).then_inc(aug_filled, 1)

            def normalise(b):
                pool.wait_ge(half_set, 1)
                pool.wait_ge(var_done, b + 1)
                nc.gpsimd.tensor_tensor(rstd[:, tiles(b)], veps[:, tiles(b)], half[:], ALU.pow).then_inc(rstd_done, 1)
                pool.wait_ge(rstd_done, b + 1)
                if b:
                    pool.wait_ge(xT_ps, b)
                for j in range(QT):
                    t = b * QT + j
                    nc.gpsimd.tensor_scalar(xn[:, j], x_sb[:, t], moments[:, t, 0:1], rstd[:, t:t + 1],
                                            ALU.subtract, ALU.mult).then_inc(xn_ready, 1)

            def split(b, w):
                i = 2 * b + w
                pool.wait_ge(rope_read, 2 * i + 2)
                if i >= 2:
                    pool.wait_ge(rest_done, i - 1)
                nc.gpsimd.tensor_tensor(rotated[:, w], rot[:, w, 0], rot[:, w, 1], ALU.add).then_inc(sum_done, 1)
                pool.wait_ge(part0_done, i + 1)
                nc.gpsimd.tensor_tensor(rest[:, w], rotated[:, w], parts[:, w, 0], ALU.subtract).then_inc(rest_done, 1)
                pool.wait_ge(part1_done, i + 1)
                pool.wait_ge(rest_done, i + 1)
                nc.gpsimd.tensor_tensor(parts[:, w, 2], rest[:, w], parts[:, w, 1], ALU.subtract).then_inc(parts_ready, 1)

            normalise(0)
            for b in range(NB):
                split(b, 0)
                if b + 1 < NB:
                    normalise(b + 1)
                split(b, 1)

            with pool.Fori(0, NB) as b:
                pool.wait_ge(v_copied, b + 1)
                pool.wait_ge(pv_done, b * NG + GRANT)
                pool.wait_ge(aug_filled, 2)
                nc.gpsimd.tensor_copy(v_aug[:, :, :, 0:D],
                                      v_all[:, ds(b * QT, QT), :].rearrange("p t (h d) -> p t h d", h=H)).then_inc(v_aug_ready, 1)

            with pool.Fori(0, NB) as b:
                pool.wait_ge(var2, b + 1)
                nc.gpsimd.tensor_tensor(rstd[:, 0:QT], veps[:, 0:QT], half[:], ALU.pow).then_inc(rstd2, 1)
                pool.wait_ge(rows_ready, b * 8 + 8)
                pool.wait_ge(place_ready, b + 1)
                pool.sem_inc(go_rows, 1)
                for j in range(QT):
                    for k in range(2):
                        nc.gpsimd.indirect_dma_start(
                            out=rows_dram, out_offset=bass.IndirectOffsetOnAxis(ap=place[:, k, j:j + 1], axis=0),
                            in_=rows[:, k, j, :], in_offset=None).then_inc(rows_sent, 16)
                pool.wait_ge(rows_sent, b * 32 * QT + 32 * QT)
                pool.sem_inc(rows_free, 1)

            with pool.Fori(0, NBLK // 4) as p:
                for k in range(4):
                    pool.wait_ge(where_done, p * 4 + k + 1)
                    pool.wait_ge(y_ready, p * 4 + k + 1)
                    pool.sem_inc(go_scatter, 1)
                    nc.gpsimd.indirect_dma_start(
                        out=y_dram, out_offset=bass.IndirectOffsetOnAxis(ap=where[:, k, :], axis=0),
                        in_=y_rows[:, k, :], in_offset=None, bounds_check=2 * NB * T - 1,
                        oob_is_err=False).then_inc(y_sent[k], 16)

        @block.scalar
        def _(act):
            act.sem_inc(exp_done, GRANT)
            act.sem_inc(heads_copied, GRANT)
            for dst, src in ((w_raw[0:L, 1], wk_up), (w_raw[0:L, 2], wv_up), (w_raw[:, 0], wq), (w_raw[:, 3], wo)):
                act.dma_start(dst, src).then_inc(w_loaded, 16)
            for dst, src in ((eye[:], c_eye), (rope[:].rearrange("p k t -> p (k t)"), c_rope)):
                act.dma_start(dst, src).then_inc(c_loaded, 16)
            for dst, src in ((eye16[:], c_eye16), (gw_sb[:], gate_w), (bias_sb[:], expert_bias.unsqueeze(0).to_broadcast([P, NE])),
                             (count[:], c_count), (expert[:], c_expert), (table_in[:], c_table), (dest[:], c_dest)):
                act.dma_start(dst, src).then_inc(r_loaded, 16)

            for b in range(NB):
                act.wait_ge(xT_ps, b + 1)
                if b:
                    act.wait_ge(v_ps, b)
                nc.scalar.copy(xT[:], ps_o[:]).then_inc(xT_copied, 1)
                for w in range(2):
                    i = 2 * b + w
                    act.wait_ge(sum_done, i + 1)
                    if b:
                        act.wait_ge(parts_saved[w], 16 * b)
                    nc.scalar.copy(parts[:, w, 0], rotated[:, w]).then_inc(part0_done, 1)
                    if w == 0:
                        act.wait_ge(v_ps, b + 1)
                        nc.scalar.copy(v_all[:, tiles(b), :].rearrange("p t e -> p (t e)"), ps_m[:]).then_inc(v_copied, 1)
                    act.wait_ge(rest_done, i + 1)
                    nc.scalar.copy(parts[:, w, 1], rest[:, w]).then_inc(part1_done, 1)

            act.wait_ge(parts_ready, 2 * NB)

            def copy_heads(b, hg):
                act.wait_ge(pv_done, b * NG + QT * (hg + 1) + GRANT)
                act.wait_ge(heads_saved[hg % 2], b * 32 + 16 * (hg // 2) + GRANT_DMA)
                nc.scalar.copy(heads_sb[:, hg % 2, :], ps_o[:]).then_inc(heads_copied, 1)

            def exponentials(b, g):
                n = T - P * (g % QT)
                act.wait_ge(pv_done, b * NG + max(g - 1, 0) + GRANT)
                for j in range(2):
                    act.wait_ge(scores_ready, b * NPAIR + 2 * g + j + 1)
                    nc.scalar.activation(prob[:, g % 2, 2 * j:2 * j + 2, 0:n], ps_b2[:, j, :, 0:n], ACT.Exp,
                                         scale=SCALE).then_inc(exp_done, 1)
                if g % QT == 0 and g > 0:
                    copy_heads(b, g // QT - 1)

            def copy_xn2T(b):
                act.wait_ge(xn2T_ps, b + 1)
                if b:
                    act.wait_ge(logits_done, b)
                nc.scalar.copy(xn2T, ps_m[:]).then_inc(xn2T_copied, 1)

            def exp_gate(b):
                act.wait_ge(gate_in, b + 1)
                nc.scalar.activation(route[:, 2], route[:, 1], ACT.Exp).then_inc(gate_exp, 1)

            with act.Fori(0, NB - 1) as b:
                for g in range(NG):
                    exponentials(b, g)
                copy_heads(b, NHG - 1)
            for g in range(NG):
                exponentials(NB - 1, g)
                for b in range(NB - 1):
                    if g == ROUTE_AT[b] + 2:
                        copy_xn2T(b)
                    if g == ROUTE_AT[b] + 3:
                        exp_gate(b)
            copy_heads(NB - 1, NHG - 1)
            copy_xn2T(NB - 1)
            exp_gate(NB - 1)

            def copy_blkT(n, k):
                act.wait_ge(blkT_ps, n + 1)
                if not (isinstance(n, int) and n < 2):
                    act.wait_ge(up_done, n - 1)
                nc.scalar.copy(blkT[:, k % 2, :], ps_o[:, 0:P]).then_inc(blkT_copied, 1)

            def silu(n, k):
                act.wait_ge(up_done, n + 1)
                if not (isinstance(n, int) and n < 2):
                    act.wait_ge(hid_done, n - 1)
                nc.scalar.activation(gate[:, k % 2, :], ps_b[:, 2 * (k % 2), 0:HID], ACT.Silu).then_inc(gate_done, 1)

            def copy_hidT(n, k):
                act.wait_ge(hidT_ps, n + 1)
                if not (isinstance(n, int) and n < 2):
                    act.wait_ge(down_done, n - 1)
                nj = HJ[2][1]
                nc.scalar.copy(hidT[:, k % 2, 0:2 * P], ps_a[:, k % 2, 0:2 * P]).then_inc(hidT_copied, 1)
                nc.scalar.copy(hidT[0:nj, k % 2, 2 * P:3 * P], ps_a[0:nj, k % 2, 2 * P:3 * P]).then_inc(hidT_copied, 1)

            def step(n, k, last=NBLK):
                late = not isinstance(n, int)
                if late or n + 1 < last:
                    copy_blkT(n + 1, k + 1)
                if late or n < last:
                    silu(n, k)
                if late or n >= 1:
                    copy_hidT(n - 1, k + 3)

            copy_blkT(0, 0)
            for n in range(4):
                step(n, n)
            with act.Fori(1, NBLK // 4 - 1) as p:
                for k in range(4):
                    step(p * 4 + k, k)
            for k in range(5):
                step(NBLK - 4 + k, k)

        @block.vector
        def _(dve):
            dve.sem_inc(shift_step, GRANT)
            def norm_stats(b):
                dve.wait_ge(x_loaded[b], 16)
                if b:
                    dve.wait_ge(moments_done, NT // NB * b)
                for j in range(QT):
                    nc.vector.bn_stats(stats[:, j, :], x_sb[:, b * QT + j, :]).then_inc(stats_done, 1)
                for j in range(QT):
                    t = b * QT + j
                    dve.wait_ge(stats_done, t + 1)
                    nc.vector.bn_aggr(moments[:, t, :], stats[:, j, :]).then_inc(moments_done, 1)
                dve.wait_ge(moments_done, QT * (b + 1))
                nc.vector.tensor_scalar(veps[:, tiles(b)], moments[:, tiles(b), 1], EPS, None, ALU.add).then_inc(var_done, 1)

            def permuted(i, src):
                v = src.rearrange("p (h i two) -> p i two h", i=D // 2, two=2)
                own = w_proj[:, i].rearrange("p (i two h) -> p i two h", i=D // 2, two=2)
                swapped = w_proj[:, i + 1].rearrange("p (i two h) -> p i two h", i=D // 2, two=2)
                for c in range(2):
                    nc.vector.tensor_copy(own[:, :, c], v[:, :, c]).then_inc(w_ready, 1)
                    nc.vector.tensor_copy(swapped[:, :, c], v[:, :, 1 - c]).then_inc(w_ready, 1)

            norm_stats(0)
            dve.wait_ge(w_loaded, 16 * 5)
            permuted(0, w_raw[:, 0])
            dve.wait_ge(wdT_ps, 1)
            nc.vector.tensor_copy(wdT[:], ps_m[0:L, 0:E]).then_inc(wdT_done, 1)
            dve.wait_ge(wkv_ps, 1)
            permuted(2, ps_m[:, 0:E])
            nc.vector.tensor_copy(w_proj[:, 4], ps_m[:, E:2 * E]).then_inc(w_ready, 1)
            dve.wait_ge(gwT_ps, 1)
            nc.vector.tensor_copy(gwT[:], ps_m[:, 2 * E:2 * E + NE]).then_inc(gwT_done, 1)
            for b in range(1, NB):
                norm_stats(b)

            def rotate(b, w):
                if b:
                    dve.wait_ge(sum_done, 2 * (b - 1) + w + 1)
                for c in range(2):
                    dve.wait_ge(proj_done, b * 4 + 2 * w + c + 1)
                    nc.vector.tensor_tensor(rot[:, w, c], ps_b[:, 2 * w + c], rope[:, c], ALU.mult).then_inc(rope_read, 1)

            m3 = negmax[:, :].rearrange("p (h q) -> p q h", q=QT)

            def maximum(b, n):
                qt, h, nh = MAX_UNITS[n]
                keys = P * (qt + 1)
                dve.wait_ge(max_scores, b * NMU + n + 1)
                nc.vector.tensor_reduce(m3[:, qt, h:h + nh],
                                        ps_a[:, n % 2, 0:nh * keys].rearrange("p (a k) -> p a k", a=nh),
                                        AXX, ALU.max, negate=True).then_inc(max_read, 1)

            def split_maxima(b):
                done = b * 4 + GRANT
                dve.wait_ge(max_read, b * NMU + NMU)
                if not isinstance(b, int):
                    dve.wait_ge(shiftT_done, b)
                nc.vector.tensor_copy(shift[:, 0], negmax[:]).then_inc(shift_step, 1)
                dve.wait_ge(shift_step, done + 1)
                nc.vector.tensor_tensor(shift_rest[:], negmax[:], shift[:, 0], ALU.subtract).then_inc(shift_step, 1)
                dve.wait_ge(shift_step, done + 2)
                nc.vector.tensor_copy(shift[:, 1], shift_rest[:]).then_inc(shift_step, 1)
                dve.wait_ge(shift_step, done + 3)
                nc.vector.tensor_tensor(shift[:, 2], shift_rest[:], shift[:, 1], ALU.subtract).then_inc(shift_step, 1)
                dve.wait_ge(shiftT_done, b + 1)
                dve.wait_ge(shift_saved, b * 16 + GRANT_DMA)
                nc.vector.tensor_copy(shiftT[:], shiftT_ps).then_inc(shiftT_copied, 1)

            dve.wait_ge(c_loaded, 16 * 2)
            rotate(0, 0)
            rotate(0, 1)
            for what, b, n in FIRST_PASS:
                if what == "max":
                    maximum(0, n)
                elif what == "q":
                    rotate(b, 0)
                elif what == "k":
                    rotate(b, 1)
            split_maxima(0)
            with dve.Fori(1, NB) as b:
                dve.wait_ge(shift_step, b * 4 + GRANT)
                for n in range(NMU):
                    maximum(b, n)
                split_maxima(b)

            dve.wait_ge(r_loaded, 16 * 7)
            per = lambda a: a.rearrange("p (t e) -> p t e", e=NE)
            over = lambda a: a.to_broadcast([P, QT, NE])
            R = [per(route[:, k]) for k in range(12)]
            largest, total, inverse = R[0][:, :, 0:1], R[0][:, :, 1:2], R[0][:, :, 2:3]
            logits = per(ps_m[:, 0:QT * NE])
            rank = per(ps_m[:, QT * NE:2 * QT * NE])
            added = ps_m[:, 2 * QT * NE:2 * QT * NE + NE]
            with dve.Fori(0, NB) as b:
                n_step = [0]

                def take_waits():
                    dve.sem_inc(go_next, 1)

                def routed(instruction):
                    n_step[0] += 1
                    instruction.then_inc(route_step, 1)
                    dve.wait_ge(route_step, b * ROUTE_STEPS + n_step[0])

                cols = ds(b * T, T)
                xb = x_sb[:, ds(b * QT, QT), :].rearrange("p t e -> p (t e)")
                dve.wait_ge(sums_loaded, b * 32 + 32)
                nc.vector.reciprocal(denom[:, cols], denom[:, cols]).then_inc(inv_done, 1)
                dve.wait_ge(inv_done, b + 1)
                nc.vector.tensor_tensor(numer[:, cols], numer[:, cols], denom[:, cols], ALU.mult).then_inc(normed, 1)
                dve.wait_ge(wo_done, b + 1)
                nc.vector.tensor_tensor(xb, ps_m[:], xb, ALU.add).then_inc(x2_ready, 1)
                dve.wait_ge(x2_ready, b + 1)
                take_waits()
                for j in range(QT):
                    nc.vector.bn_stats(stats[:, j, :], x_sb[:, ds(b * QT + j, 1), :].rearrange("p a e -> p (a e)")).then_inc(stats2, 1)
                dve.wait_ge(stats2, b * QT + QT)
                take_waits()
                for j in range(QT):
                    nc.vector.bn_aggr(moments[:, j, :], stats[:, j, :]).then_inc(moments2, 1)
                dve.wait_ge(moments2, b * QT + QT)
                nc.vector.tensor_scalar(veps[:, 0:QT], moments[:, 0:QT, 1], EPS, None, ALU.add).then_inc(var2, 1)
                dve.wait_ge(rstd2, b + 1)
                for j in range(QT):
                    nc.vector.tensor_scalar(xn2[:, j], x_sb[:, ds(b * QT + j, 1), :].rearrange("p a e -> p (a e)"),
                                            moments[:, j, 0:1], rstd[:, j:j + 1], ALU.subtract, ALU.mult).then_inc(xn2_ready, 1)

                dve.wait_ge(logits_done, b + 1)
                routed(nc.vector.tensor_reduce(largest, logits, AXX, ALU.max))
                nc.vector.tensor_tensor(R[1], logits, over(largest), ALU.subtract).then_inc(gate_in, 1)
                dve.wait_ge(gate_exp, b + 1)
                routed(nc.vector.tensor_reduce(total, R[2], AXX, ALU.add))
                routed(nc.vector.reciprocal(inverse, total))
                routed(nc.vector.tensor_tensor(R[3], R[2], over(inverse), ALU.mult))
                routed(nc.vector.tensor_tensor(R[4], R[3], bias_sb[:].unsqueeze(1).to_broadcast([P, QT, NE]), ALU.add))
                take_waits()
                for j in range(QT):
                    nc.vector.max(R[5][:, j], R[4][:, j]).then_inc(best_found, 1)
                dve.wait_ge(best_found, b * 2 * QT + QT)
                take_waits()
                for j in range(QT):
                    nc.vector.max_index(R[6][:, j].bitcast(U32), R[5][:, j], R[4][:, j]).then_inc(best_found, 1)
                dve.wait_ge(best_found, b * 2 * QT + 2 * QT)
                routed(nc.vector.tensor_copy(route[:, 7], route[:, 6].bitcast(U32)))
                for k in range(2):
                    routed(nc.vector.tensor_tensor(R[8 + k], expert[:, 0:1, :].to_broadcast([P, QT, NE]),
                                                   over(R[7][:, :, k:k + 1]), ALU.is_equal))
                nc.vector.tensor_tensor(taken[:], route[:, 8], route[:, 9], ALU.add).then_inc(taken_ready, 1)
                for k in range(2):
                    routed(nc.vector.tensor_tensor(R[10], R[8 + k], R[3], ALU.mult))
                    routed(nc.vector.tensor_reduce(picked[:, 0, k], R[10], AXX, ALU.add))
                dve.wait_ge(rows_free, b + GRANT)
                routed(nc.vector.tensor_copy(rows[:, :, :, E].bitcast(I32), dest[:, ds(b * QT, QT), :].rearrange("p t k -> p k t")))
                for j in range(QT):
                    for k in range(2):
                        nc.vector.tensor_scalar(rows[:, k, j, 0:E], xn2[:, j], picked[:, 0, k, j:j + 1], None,
                                                ALU.mult).then_inc(rows_ready, 1)
                dve.wait_ge(ranked, b + 1)
                routed(nc.vector.tensor_tensor(R[11], rank, expert[:, 1:2, :].to_broadcast([P, QT, NE]), ALU.add))
                routed(nc.vector.tensor_tensor(expert[:, 1], expert[:, 1], added, ALU.add))
                for k in range(2):
                    routed(nc.vector.tensor_tensor(R[10], R[8 + k], R[11], ALU.mult))
                    routed(nc.vector.tensor_reduce(picked[:, 1, k], R[10], AXX, ALU.add))
                nc.vector.tensor_copy(place[:], picked[:, 1]).then_inc(place_ready, 1)
                assert n_step[0] == ROUTE_STEPS, n_step[0]

            n_table = [0]

            def tabled(instruction):
                n_table[0] += 1
                instruction.then_inc(table_step, 1)
                dve.wait_ge(table_step, n_table[0])

            n0 = NBLK * NE
            block_no = table_in[:, 0:n0].rearrange("p (n e) -> p n e", e=NE)
            up_to = table_in[:, n0:n0 + NE * NE].rearrange("p (e f) -> p e f", e=NE)
            first_row = table_in[:, n0 + NE * NE:n0 + NE * NE + NE]
            block_no1 = table_in[:, n0 + NE * NE + NE:]
            wide = [tables[:, k].rearrange("p (n e) -> p n e", e=NE) for k in range(2)]
            S = [short[:, k] for k in range(8)]
            e1 = lambda k: S[k][:, 0:NE]
            nc.vector.tensor_copy(free_row[:], expert[0:1, 1]).then_inc(table_ready, 1)
            tabled(nc.vector.tensor_tensor(e1(0), expert[0:1, 1], first_row, ALU.subtract))
            tabled(nc.vector.tensor_scalar(e1(1).bitcast(I32), e1(0), float(P - 1), None, ALU.add))
            tabled(nc.vector.tensor_scalar(e1(2).bitcast(I32), e1(1).bitcast(I32), P.bit_length() - 1, None, ALU.logical_shift_right))
            tabled(nc.vector.tensor_copy(e1(3), e1(2).bitcast(I32)))
            in_blocks = e1(3)
            tabled(nc.vector.tensor_tensor(wide[0][:, 0:NE], up_to, in_blocks.unsqueeze(1).to_broadcast([1, NE, NE]), ALU.mult))
            tabled(nc.vector.tensor_reduce(e1(4), wide[0][:, 0:NE], AXX, ALU.add))
            tabled(nc.vector.tensor_tensor(wide[0], block_no, e1(4).unsqueeze(1).to_broadcast([1, NBLK, NE]), ALU.is_ge))
            tabled(nc.vector.tensor_reduce(S[5], wide[0], AXX, ALU.add))
            tabled(nc.vector.tensor_tensor(wide[1], wide[0], in_blocks.unsqueeze(1).to_broadcast([1, NBLK, NE]), ALU.mult))
            tabled(nc.vector.tensor_reduce(S[6], wide[1], AXX, ALU.add))
            tabled(nc.vector.tensor_tensor(S[7], block_no1, S[6], ALU.subtract))
            tabled(nc.vector.tensor_scalar(S[0], S[5], float(NE), float(P), ALU.is_lt, ALU.mult))
            tabled(nc.vector.tensor_tensor(S[1], S[7], S[0], ALU.mult))
            tabled(nc.vector.tensor_scalar(S[2], S[5], float(REGION), None, ALU.mult))
            tabled(nc.vector.tensor_tensor(block_table[:, 0], S[1], S[2], ALU.add))
            nc.vector.tensor_scalar(block_table[:, 1], S[5], float(NE - 1), None, ALU.min).then_inc(table_ready, 1)

            def keep_where(p, k):
                dve.wait_ge(blk_loaded[k], p * 16 + 16)
                if not (isinstance(p, int) and p == 0):
                    dve.wait_ge(y_sent[k], p * 16)
                nc.vector.tensor_copy(where[:, k, :], blk[:, k, E:E + 1].bitcast(U32)).then_inc(where_done, 1)

            def product(n, k):
                dve.wait_ge(gate_done, n + 1)
                if not (isinstance(n, int) and n < 2):
                    dve.wait_ge(hidT_ps, n - 1)
                nc.vector.tensor_tensor(hid[:, k % 2, :], ps_b[:, 2 * (k % 2) + 1, 0:HID], gate[:, k % 2, :],
                                        ALU.mult).then_inc(hid_done, 1)

            def result(n, k):
                dve.wait_ge(down_done, n + 1)
                nc.vector.tensor_copy(y_rows[:, k % 4, :], ps_m[:, 0:E]).then_inc(y_ready, 1)

            def step(p, k, n_last=NBLK):
                n = p * 4 + k
                if not isinstance(n, int) or n < n_last:
                    keep_where(p, k)
                    product(n, k)
                if not isinstance(n, int) or n >= 2:
                    result(n - 2, k + 2)

            for k in range(4):
                step(0, k)
            with dve.Fori(1, NBLK // 4 - 1) as p:
                for k in range(4):
                    step(p, k)
            for k in range(6):
                step(NBLK // 4 - 1, k)

            for b in range(NB):
                dve.wait_ge(y_loaded[b], 32)
                nc.vector.tensor_tensor(x_sb[:, tiles(b), :], x_sb[:, tiles(b), :], y_sb[:, 0, tiles(b), :], ALU.add).then_inc(y_added, 1)
                dve.wait_ge(y_added, b + 1)
                nc.vector.tensor_tensor(x_sb[:, tiles(b), :], x_sb[:, tiles(b), :], y_sb[:, 1, tiles(b), :], ALU.add).then_inc(out_ready, 1)

        @block.tensor
        def _(pe):
            pe.sem_inc(pv_done, GRANT)
            pe.wait_ge(w_loaded, 16 * 5)
            pe.wait_ge(c_loaded, 16 * 2)
            nc.tensor.transpose(ps_m[0:L, 0:E], wd_sb[:], eye[:]).then_inc(wdT_ps, 1)
            pe.wait_ge(wdT_done, 1)
            nc.tensor.matmul(ps_m[:, 0:E], wdT[:], w_raw[0:L, 1], start=True, stop=True)
            nc.tensor.matmul(ps_m[:, E:2 * E], wdT[:], w_raw[0:L, 2], start=True, stop=True).then_inc(wkv_ps, 1)
            pe.wait_ge(r_loaded, 16 * 7)
            pe.wait_ge(w_ready, 9)
            nc.tensor.transpose(ps_m[:, 2 * E:2 * E + NE], gw_sb[:], eye[0:NE, 0:NE]).then_inc(gwT_ps, 1)

            def turn_x(b):
                pe.wait_ge(xn_ready, b * QT + QT)
                if b:
                    pe.wait_ge(xT_copied, b)
                for j in range(QT):
                    last = nc.tensor.transpose(ps_o[:, j * P:(j + 1) * P], xn[:, j, :], eye[:])
                last.then_inc(xT_ps, 1)

            def project(b, w):
                pe.wait_ge(xT_copied, b + 1)
                if b:
                    pe.wait_ge(rope_read, 4 * (b - 1) + 2 * w + 2)
                for i in range(2 * w, 2 * w + 2):
                    nc.tensor.matmul(ps_b[:, i], w_proj[:, i], xT[:], start=True, stop=True).then_inc(proj_done, 1)

            def project_v(b):
                pe.wait_ge(gwT_done, 1)
                if b:
                    pe.wait_ge(v_copied, b)
                for j in range(QT):
                    last = nc.tensor.matmul(ps_m[:, j * P:(j + 1) * P], xT[:, j * P:(j + 1) * P], w_proj[:, 4], start=True, stop=True)
                last.then_inc(v_ps, 1)

            def qs(b, h, t0, n, rows):
                return q_stack[0:rows, b, h * T + t0:h * T + t0 + n]

            def ks(b, h, t0, n, rows):
                return k_stack[0:rows, b, h * T + t0:h * T + t0 + n]

            def max_unit(b, n):
                qt, h0, nh = MAX_UNITS[n]
                keys = P * (qt + 1)
                if not isinstance(b, int):
                    pe.wait_ge(max_read, b * NMU + n - 1)
                elif n >= 2:
                    pe.wait_ge(max_read, n - 1)
                for a in range(nh):
                    last = nc.tensor.matmul(ps_a[:, n % 2, a * keys:(a + 1) * keys], qs(b, h0 + a, qt * P, P, SHIFT_ROW),
                                            ks(b, h0 + a, 0, keys, SHIFT_ROW), start=True, stop=True)
                last.then_inc(max_scores, 1)

            def transpose_shift(b):
                pe.wait_ge(shift_step, b * 4 + 4 + GRANT)
                if isinstance(b, int):
                    pe.wait_ge(v_copied, NB)
                else:
                    pe.wait_ge(shiftT_copied, b)
                for k in range(2):
                    last = nc.tensor.transpose(shiftT_ps[:, k, :], shift_cols[:, k * SR:(k + 1) * SR], eye16[:])
                last.then_inc(shiftT_done, 1)

            def scores(b, g, j):
                hg, kt = divmod(g, QT)
                if g == 0 and j == 0:
                    pe.wait_ge(shift_loaded, b * 16 + 16)
                u = 2 * g + j
                pe.wait_ge(exp_done, b * NPAIR + max(u - 1, 0) + GRANT)
                for a in range(2):
                    h = HG * hg + 2 * j + a
                    last = nc.tensor.matmul(ps_b2[:, j, a, 0:T - kt * P], ks(b, h, kt * P, P, ROWS),
                                            qs(b, h, kt * P, T - kt * P, ROWS), start=True, stop=True)
                last.then_inc(scores_ready, 1)

            def values(b, g):
                hg, kt = divmod(g, QT)
                pe.wait_ge(exp_done, b * NPAIR + 2 * g + 2 + GRANT)
                if g == 0:
                    pe.wait_ge(v_aug_ready, b + 1)
                if kt == 0:
                    pe.wait_ge(heads_copied, b * NHG + hg + GRANT)
                for a in range(HG):
                    last = nc.tensor.matmul(ps_o[a * AUG:(a + 1) * AUG, kt * P:T], v_aug[:, kt, HG * hg + a, :],
                                            prob[:, g % 2, a, 0:T - kt * P], start=kt == 0, stop=kt == QT - 1)
                last.then_inc(pv_done, 1)

            turn_x(0)
            project(0, 0)
            project(0, 1)
            project_v(0)
            pe.wait_ge(rows_loaded, 16 * 2 * NB)
            for what, b, n in FIRST_PASS:
                if what == "max":
                    if n == 0:
                        pe.wait_ge(stack_loaded[0], STACK_DMAS)
                    max_unit(0, n)
                elif what == "x":
                    turn_x(b)
                elif what == "q":
                    project(b, 0)
                elif what == "k":
                    project(b, 1)
                else:
                    project_v(b)
            transpose_shift(0)
            pe.wait_ge(rope_read, 4 * NB)
            for b in range(1, NB):
                pe.wait_ge(stack_loaded[b], STACK_DMAS)
            with pe.Fori(1, NB) as b:
                n = 0
                for g in range(NG):
                    want = min(NMU, AHEAD + (NMU - AHEAD) * g // (NG - 1))
                    for j in range(2):
                        mid = want if j or g == 0 else (n + want) // 2
                        while n < mid:
                            max_unit(b, n)
                            n += 1
                        scores(b - 1, g, j)
                    if g:
                        values(b - 1, g - 1)
                values(b - 1, NG - 1)
                transpose_shift(b)

            def out_project(b):
                pe.wait_ge(normed, b + 1)
                if b:
                    pe.wait_ge(route_step, b * ROUTE_STEPS)
                else:
                    pe.wait_ge(shiftT_copied, NB)
                for j in range(QT):
                    last = nc.tensor.matmul(ps_m[:, j * P:(j + 1) * P], numer[:, (b * QT + j) * P:(b * QT + j + 1) * P],
                                            w_raw[:, 3], start=True, stop=True)
                last.then_inc(wo_done, 1)

            def turn_xn2(b):
                pe.wait_ge(xn2_ready, QT * (b + 1))
                for j in range(QT):
                    last = nc.tensor.transpose(ps_m[:, j * P:(j + 1) * P], xn2[:, j, :], eye[:])
                last.then_inc(xn2T_ps, 1)

            def gate_logits(b):
                pe.wait_ge(xn2T_copied, b + 1)
                for j in range(QT):
                    last = nc.tensor.matmul(ps_m[:, j * NE:(j + 1) * NE], xn2T[:, j * P:(j + 1) * P], gwT[:], start=True, stop=True)
                last.then_inc(logits_done, 1)

            def ranks(b):
                pe.wait_ge(taken_ready, b + 1)
                r0, n = QT * NE, QT * NE
                for i in range(QT):
                    here = ps_m[:, r0 + i * NE:r0 + (i + 1) * NE]
                    nc.tensor.matmul(here, count[:, 0], taken[:, i * NE:(i + 1) * NE], start=True, stop=(i == 0))
                    for j in range(i):
                        nc.tensor.matmul(here, count[:, 1], taken[:, j * NE:(j + 1) * NE], start=False, stop=(j == i - 1))
                for j in range(QT):
                    last = nc.tensor.matmul(ps_m[:, r0 + n:r0 + n + NE], count[:, 1], taken[:, j * NE:(j + 1) * NE],
                                            start=(j == 0), stop=(j == QT - 1))
                last.then_inc(ranked, 1)

            for g in range(NG):
                for j in range(2):
                    scores(NB - 1, g, j)
                if g:
                    values(NB - 1, g - 1)
                for b in range(NB - 1):
                    for k, stage in enumerate((out_project, turn_xn2, gate_logits, ranks)):
                        if g == min(ROUTE_AT[b] + (0, 2, 3, 5)[k], NG - 1):
                            stage(b)
            values(NB - 1, NG - 1)
            for stage in (out_project, turn_xn2, gate_logits, ranks):
                stage(NB - 1)

            def turn_blk(n, k):
                if isinstance(n, int) and n < 4:
                    pe.wait_ge(blk_loaded[k % 4], 16)
                elif isinstance(n, int):
                    pe.wait_ge(blk_loaded[k % 4], 16 * (n // 4 + 1))
                else:
                    pe.wait_ge(blk_loaded[k % 4], n * 4 - (k % 4) * 4 + 16)
                if not (isinstance(n, int) and n == 0):
                    pe.wait_ge(blkT_copied, n)
                nc.tensor.transpose(ps_o[:, 0:P], blk[:, k % 4, 0:E], eye[:]).then_inc(blkT_ps, 1)

            def expert_of(n):
                return pe.value_load(block_table[0:1, 1, ds(n, 1)], min_val=0, max_val=NE - 1)

            def up(n, k):
                e = expert_of(n)
                pe.wait_ge(blkT_copied, n + 1)
                if not (isinstance(n, int) and n < 2):
                    pe.wait_ge(gate_done, n - 1)
                    pe.wait_ge(hid_done, n - 1)
                for w in range(2):
                    last = nc.tensor.matmul(ps_b[:, 2 * (k % 2) + w, 0:HID], blkT[:, k % 2, :], w13[:, ds(e, 1), w, :],
                                            start=True, stop=True)
                last.then_inc(up_done, 1)

            def turn_hid(n, k):
                pe.wait_ge(hid_done, n + 1)
                if not (isinstance(n, int) and n < 2):
                    pe.wait_ge(hidT_copied, n * 2 - 2)
                for j, (j0, nj) in enumerate(HJ):
                    last = nc.tensor.transpose(ps_a[0:nj, k % 2, j * P:(j + 1) * P], hid[:, k % 2, j0:j0 + nj], eye[:])
                last.then_inc(hidT_ps, 1)

            def down(n, k):
                e = expert_of(n)
                pe.wait_ge(hidT_copied, n * 2 + 2)
                if not (isinstance(n, int) and n == 0):
                    pe.wait_ge(y_ready, n)
                for j, (j0, nj) in enumerate(HJ):
                    last = nc.tensor.matmul(ps_m[:, 0:E], hidT[0:nj, k % 2, j * P:(j + 1) * P], w2_sb[0:nj, ds(e, 1), j, :],
                                            start=(j == 0), stop=(j == 2))
                last.then_inc(down_done, 1)

            def step(n, k, last=NBLK):
                late = not isinstance(n, int)
                if late or n + 1 < last:
                    turn_blk(n + 1, k + 1)
                if late or n < last:
                    up(n, k)
                if late or 1 <= n <= last:
                    turn_hid(n - 1, k + 3)
                if late or n >= 2:
                    down(n - 2, k + 2)

            pe.wait_ge(experts_loaded, 16 * 5)
            pe.wait_ge(table_ready, 2)
            turn_blk(0, 0)
            for n in range(4):
                step(n, n)
            with pe.Fori(1, NBLK // 4 - 1) as p:
                for k in range(4):
                    step(p * 4 + k, k)
            for k in range(6):
                step(NBLK - 4 + k, k)


FIRST_PASS = []
for _n in range(NMU):
    FIRST_PASS.append(("max", 0, _n))
    for _b in range(1, NB):
        for _k, _what in enumerate("xqkv"):
            if _n == 2 + 13 * (_b - 1) + (0, 3, 5, 7)[_k]:
                FIRST_PASS.append((_what, _b, 0))
AHEAD = 8
ROUTE_AT = (0, 5, 10)
ROUTE_STEPS = 5 + 1 + 2 + 4 + 1 + 2 + 4
STACK_DMAS = 16 * 2 * PARTS

_INS = ["L0_attn_x", "L0_attn_wq", "L0_attn_w_down", "L0_attn_wk_up", "L0_attn_wv_up", "L0_attn_wo",
        "L0_ffn_gate_w", "L0_ffn_expert_bias", "L0_ffn_w1", "L0_ffn_w2", "L0_ffn_w3"]


def kernel(**inputs):
    import concourse.bacc as bacc
    from concourse.bass_utils import run_bass_kernel_spmd

    nc = bacc.Bacc("TRN2", target_bir_lowering=False, num_devices=1)
    arrays, args = {}, []
    for name in _INS:
        a = np.ascontiguousarray(inputs[name])
        arrays[name] = a
        args.append(nc.dram_tensor(name, a.shape, mybir.dt.from_np(a.dtype), kind="ExternalInput").ap())
    out = nc.dram_tensor("out", (NB, T, E), F32, kind="ExternalOutput").ap()
    consts = {}
    for name, a in constants().items():
        arrays[name] = a
        consts[name] = nc.dram_tensor(name, a.shape, mybir.dt.from_np(a.dtype), kind="ExternalInput").ap()
    build_block(nc, *args, out, **consts)
    r = run_bass_kernel_spmd(nc, [arrays], core_ids=[0])
    return r.results[0]["out"]
```

```python
from contextlib import ExitStack

import numpy as np

import concourse.bass as bass
from concourse import mybir

F32 = mybir.dt.float32
BF16 = mybir.dt.bfloat16
U32 = mybir.dt.uint32
I32 = mybir.dt.int32
ALU = mybir.AluOpType
ACT = mybir.ActivationFunctionType
AXX = mybir.AxisListType.X

P = 128
NB, T, E = 4, 512, 128
H = 16
D = E // H
L = E // 2
PAGE = 32
NPAGE = T // PAGE
QT = T // P
NT = NB * QT
EPS = 1e-5
SCALE = 1.0 / float(np.sqrt(D))

PARTS = 3
MASK_ROW = PARTS * PARTS * D
SHIFT_ROW = MASK_ROW + NPAGE
ROWS = SHIFT_ROW + PARTS
BIG = 2.0 ** 126

SR = PARTS * H * QT // 2

HG = 4
NHG = H // HG
AUG = 32

NE, HID = 8, 352
HJ = [(0, 128), (128, 128), (256, 96)]

REGION = NB * T + P
NBLK = -(-(2 * NB * T + NE * (P - 1)) // P)
NBLK += -NBLK % 4
NQ = NBLK // 4
ROW = E + 1
NOWHERE = 1 << 20

MAX_UNITS = ([(3, h, 1) for h in range(H)] + [(2, h, 1) for h in range(H)]
             + [(1, h, 2) for h in range(0, H, 2)] + [(0, h, 4) for h in range(0, H, 4)])
NMU = len(MAX_UNITS)
NG = NHG * QT
NPAIR = 2 * NG


def constants():
    bf = mybir.dt.np(BF16)
    inv = 1.0 / 10000.0 ** (np.arange(0, D, 2, dtype=np.float32) / D)
    ang = np.outer(np.arange(T, dtype=np.float32), inv)
    cos, sin = np.cos(ang).astype(np.float32).T, np.sin(ang).astype(np.float32).T
    rope = np.empty((D, H, 2, T), np.float32)
    for d in range(D):
        rope[d, :, 0] = cos[d // 2]
        rope[d, :, 1] = sin[d // 2] if d % 2 else -sin[d // 2]
    page = np.arange(T) // PAGE
    rows = np.arange(NPAGE)[:, None]
    k_rows = np.concatenate([(page[None] == rows), np.ones((PARTS, T))]).astype(np.float32)
    q_rows = np.where(page[None] < rows, -BIG, 0.0).astype(np.float32)
    pad = np.zeros((P, ROW), np.float32)
    pad.view(np.int32)[:, E] = NOWHERE
    return {
        "c_rope": rope.reshape(P, 2 * T),
        "c_krows": k_rows.astype(bf),
        "c_qrows": q_rows.astype(bf),
        "c_eye": np.eye(P, dtype=np.float32),
        "c_eye16": np.eye(P).astype(bf),
        "c_count": np.stack([np.triu(np.ones((P, P)), 1), np.ones((P, P))], 1).astype(bf),
        "c_expert": np.tile(np.stack([np.arange(NE), REGION * np.arange(NE)]).astype(np.float32), (P, 1, 1)),
        "c_table": np.concatenate([
            np.repeat(np.arange(NBLK), NE), np.tril(np.ones((NE, NE))).ravel(), REGION * np.arange(NE),
            np.arange(NBLK), np.repeat([8.0 ** np.arange(2, 6), [0, 0, 1, 8]], NQ, 0).ravel()]).astype(np.float32)[None],
        "c_dest": (np.arange(2)[None, None] * NB * T + np.arange(NT)[None, :, None] * P
                   + np.arange(P)[:, None, None]).astype(np.int32),
        "c_pad": pad,
    }


def build_block(nc, x, wq, w_down, wk_up, wv_up, wo, gate_w, expert_bias, w1, w2, w3, out,
                c_rope, c_krows, c_qrows, c_eye, c_eye16, c_count, c_expert, c_table, c_dest, c_pad):
    ds = bass.ds
    with ExitStack() as ctx:
        def sb(name, shape, dt=F32):
            return ctx.enter_context(nc.sbuf_tensor(name, shape, dt))

        def ps(name, shape, dt=F32):
            return ctx.enter_context(nc.psum_tensor(name, shape, dt))

        def sem(name):
            return ctx.enter_context(nc.semaphore(name))

        parts_dram = nc.dram_tensor("parts_dram", (NB, 2, PARTS, P, T), BF16, kind="Internal").ap()
        shift_dram = nc.dram_tensor("shift_dram", (NB, PARTS * H * QT, P), BF16, kind="Internal").ap()
        heads_dram = nc.dram_tensor("heads_dram", (NB, NHG * P, T), F32, kind="Internal").ap()
        rows_dram = nc.dram_tensor("rows_dram", ((NE + 1) * REGION, ROW), F32, kind="Internal").ap()
        y_dram = nc.dram_tensor("y_dram", (2 * NB * T, E), F32, kind="Internal").ap()

        stack = sb("stack", [P, 2, NB, H * T], BF16)
        q_stack, k_stack = stack[:, 0], stack[:, 1]
        x_sb = sb("x_sb", [P, NT, E])
        xn = sb("xn", [P, QT, E])
        split_area = sb("split_area", [P, 4, T])
        v_all = sb("v_all", [P, NT, E])
        v_aug = sb("v_aug", [P, QT, H, AUG])
        work = sb("work", [P, 8 * T])
        rope = sb("rope", [P, 2, T])
        parts = sb("parts", [P, 2, PARTS, T], BF16)
        xT = sb("xT", [P, T])
        heads_sb = sb("heads_sb", [P, 2, T])
        w_raw = sb("w_raw", [P, 4, E])
        wd_sb = sb("wd_sb", [P, L])
        wdT = sb("wdT", [L, E])
        w_proj = sb("w_proj", [P, 5, E])
        eye = sb("eye", [P, P])
        eye16 = sb("eye16", [P, P], BF16)
        count = sb("count", [P, 2, P], BF16)
        half = sb("half", [P, QT])
        stats = sb("stats", [P, QT, 6])
        moments = sb("moments", [P, NT, 2])
        veps = sb("veps", [P, NT])
        rstd = sb("rstd", [P, NT])
        negmax = sb("negmax", [P, H * QT])
        shift_rest = sb("shift_rest", [P, H * QT])
        shift = sb("shift", [P, PARTS, H * QT], BF16)
        shiftT = sb("shiftT", [SR, 2, P], BF16)
        gw_sb = sb("gw_sb", [NE, E])
        gwT = sb("gwT", [P, NE])
        bias_sb = sb("bias_sb", [P, NE])
        expert = sb("expert", [P, 2, NE])
        dest = sb("dest", [P, NT, 2], I32)
        table_in = sb("table_in", [1, NBLK * NE + NE * NE + NE + 3 * NBLK])
        free_row = sb("free_row", [1, NE], I32)
        first_rows = sb("first_rows", [1, NBLK], I32)
        experts = sb("experts", [1, NQ], I32)
        route = sb("route", [P, 12, QT * NE])
        taken = sb("taken", [P, QT * NE], BF16)
        picked = sb("picked", [P, 4, 2, QT])
        place = sb("place", [P, 2, QT], U32)

        rot, rotated, rest = split_area[:, 0:2], split_area[:, 2], split_area[:, 3]
        prob = work[:, :].rearrange("p (s g t) -> p s g t", s=2, g=HG)
        tables = work[0:1, 0:2 * NBLK * NE].rearrange("p (k n) -> p k n", k=2)
        short = work[0:1, 2 * NBLK * NE:(2 * NE + 8) * NBLK].rearrange("p (k n) -> p k n", k=8)
        cut = [0]

        def of_work(*dims):
            a = cut[0]
            cut[0] += int(np.prod(dims))
            assert cut[0] <= 8 * T
            v = work[:, a:cut[0]]
            return v.rearrange("p (s n) -> p s n", s=dims[0])

        blk = of_work(4, ROW)
        blkT = of_work(2, P)
        gate = of_work(2, HID)
        hid = of_work(2, HID)
        hidT = of_work(2, 3 * P)
        y_rows = of_work(4, E)
        where = of_work(4, 1).bitcast(U32)
        xn2 = rope[:, 0, :].rearrange("p (t e) -> p t e", e=E)
        xn2T = rope[:, 1, :]
        rows = parts[:, :, :, :].rearrange("p w k t -> p (w k t)").bitcast(F32)[:, 0:2 * QT * ROW].rearrange(
            "p (k t n) -> p k t n", k=2, t=QT)
        area = stack[:, :, :, :].rearrange("p w b n -> p (w b n)").bitcast(F32)
        SEQ = H * T // 2
        numer, denom = area[:, 0:NB * T], area[:, NB * T:2 * NB * T]
        assert 2 * NB * T <= SEQ and NE * HID <= SEQ
        k_area = area[:, NB * SEQ:]
        w2_sb = k_area[:, 0:NE * 3 * E].rearrange("p (e j n) -> p e j n", e=NE, j=3)
        w13 = [a[:, SEQ:SEQ + NE * HID].rearrange("p (e n) -> p e n", e=NE) for a in (area, k_area)]
        y_sb = area[:, 2 * SEQ:3 * SEQ].rearrange("p (k t e) -> p k t e", k=2, e=E)
        assert NE * 3 * E <= SEQ and 2 * NT * E <= SEQ

        ps_a = ps("ps_a", [P, 2, T])
        ps_b = ps("ps_b", [P, 4, T])
        ps_o = ps("ps_o", [P, T])
        ps_m = ps("ps_m", [P, T])
        ps_b2 = ps_b[:, :, :].rearrange("p (s w) t -> p s w t", s=2)
        shiftT_ps = ps_m[0:SR, 0:P].bitcast(BF16).rearrange("p (k q) -> p k q", k=2)
        shift_cols = shift[:, :, :].rearrange("p k c -> p (k c)")

        GRANT, GRANT_DMA = 1, 16
        x_loaded = [sem(f"x_loaded{b}") for b in range(NB)]
        w_loaded, c_loaded, r_loaded = sem("w_loaded"), sem("c_loaded"), sem("r_loaded")
        rows_loaded = sem("rows_loaded")
        stats_done, moments_done, var_done = sem("stats_done"), sem("moments_done"), sem("var_done")
        half_set, rstd_done, xn_ready = sem("half_set"), sem("rstd_done"), sem("xn_ready")
        wdT_ps, wdT_done, wkv_ps, w_ready = sem("wdT_ps"), sem("wdT_done"), sem("wkv_ps"), sem("w_ready")
        xT_ps, xT_copied = sem("xT_ps"), sem("xT_copied")
        proj_done, rope_read = sem("proj_done"), sem("rope_read")
        v_ps, v_copied = sem("v_ps"), sem("v_copied")
        sum_done, part0_done, rest_done, part1_done = sem("sum_done"), sem("part0_done"), sem("rest_done"), sem("part1_done")
        parts_ready = sem("parts_ready")
        parts_saved = [sem("q_parts_saved"), sem("k_parts_saved")]
        stack0_loaded, stack_loaded = sem("stack0_loaded"), sem("stack_loaded")
        max_scores, max_read = sem("max_scores"), sem("max_read")
        shift_step = sem("shift_step")
        shiftT_done, shiftT_copied = sem("shiftT_done"), sem("shiftT_copied")
        shift_saved, shift_loaded = sem("shift_saved"), sem("shift_loaded")
        aug_filled, v_aug_ready = sem("aug_filled"), sem("v_aug_ready")
        scores_ready, exp_done, pv_done = sem("scores_ready"), sem("exp_done"), sem("pv_done")
        heads_copied = sem("heads_copied")
        heads_saved = [sem("heads_saved0"), sem("heads_saved1")]
        sums_loaded = sem("sums_loaded")
        experts_loaded, pad_saved = sem("experts_loaded"), sem("pad_saved")
        gwT_ps, gwT_done = sem("gwT_ps"), sem("gwT_done")
        inv_done, normed, wo_done, x2_ready = sem("inv_done"), sem("normed"), sem("wo_done"), sem("x2_ready")
        stats2, moments2, var2, rstd2 = sem("stats2"), sem("moments2"), sem("var2"), sem("rstd2")
        xn2_ready, xn2T_ps, xn2T_copied = sem("xn2_ready"), sem("xn2T_ps"), sem("xn2T_copied")
        logits_done, route_step, gate_in, gate_exp = sem("logits_done"), sem("route_step"), sem("gate_in"), sem("gate_exp")
        taken_ready, ranked, rows_ready, place_ready = sem("taken_ready"), sem("ranked"), sem("rows_ready"), sem("place_ready")

        best_found = sem("best_found")
        rows_sent = sem("rows_sent")
        table_step, table_ready = sem("table_step"), sem("table_ready")
        blk_loaded = [sem(f"blk_loaded{k}") for k in range(4)]
        where_done, blkT_ps, blkT_copied = sem("where_done"), sem("blkT_ps"), sem("blkT_copied")
        up_done, gate_done, hid_done = sem("up_done"), sem("gate_done"), sem("hid_done")
        hidT_ps, hidT_copied, down_done, y_ready = sem("hidT_ps"), sem("hidT_copied"), sem("down_done"), sem("y_ready")
        go_load, go_scatter = sem("go_load"), sem("go_scatter")
        y_sent = [sem(f"y_sent{k}") for k in range(4)]
        y_loaded = [sem(f"y_loaded{b}") for b in range(NB)]
        y_added, out_ready, out_saved = sem("y_added"), sem("out_ready"), sem("out_saved")

        block = ctx.enter_context(nc.Block())

        x_tiles = x.rearrange("b (t p) e -> p (b t) e", p=P)
        out_tiles = out.rearrange("b (t p) e -> p (b t) e", p=P)

        def tiles(b):
            return slice(QT * b, QT * (b + 1))

        @block.sync
        def _(sp):
            sp.sem_inc(shift_saved, GRANT_DMA)
            for s in range(2):
                sp.sem_inc(heads_saved[s], GRANT_DMA)
            for b in range(2):
                sp.dma_start(x_sb[:, tiles(b), :], x_tiles[:, tiles(b), :]).then_inc(x_loaded[b], 16)
                if b == 0:
                    sp.dma_start(wd_sb[:], w_down).then_inc(w_loaded, 16)
            for b in range(NB):
                sp.dma_start(q_stack[MASK_ROW:SHIFT_ROW, b, :].rearrange("p (h t) -> p h t", h=H),
                             c_qrows.unsqueeze(1).to_broadcast([NPAGE, H, T])).then_inc(rows_loaded, 16)
                sp.dma_start(k_stack[MASK_ROW:ROWS, b, :].rearrange("p (h t) -> p h t", h=H),
                             c_krows.unsqueeze(1).to_broadcast([NPAGE + PARTS, H, T])).then_inc(rows_loaded, 16)

            for b in range(2, NB):
                sp.dma_start(x_sb[:, tiles(b), :], x_tiles[:, tiles(b), :]).then_inc(x_loaded[b], 16)

            def stack_parts(b, w):
                sp.wait_ge(parts_ready, b * 2 + w + 1)
                sp.dma_start(parts_dram[b, w].rearrange("k p t -> p k t"), parts[:, w]).then_inc(parts_saved[w], 16)
                sp.wait_ge(parts_saved[w], b * 16 + 16)
                part = parts_dram[b, w].rearrange("k (d h) t -> k d (h t)", d=D)
                loaded = stack0_loaded if isinstance(b, int) and b == 0 else stack_loaded
                for k in range(PARTS):
                    r0 = PARTS * D * k
                    if w == 0:
                        sp.dma_start(q_stack[r0:r0 + PARTS * D, b, :],
                                     part[k:k + 1].to_broadcast([PARTS, D, H * T])).then_inc(loaded, 16)
                    else:
                        sp.dma_start(k_stack[r0:r0 + PARTS * D, b, :],
                                     part.rearrange("k d n -> (k d) n")).then_inc(loaded, 16)

            for b in range(2):
                for w in range(2):
                    stack_parts(b, w)

            def load_shift(b):
                sp.wait_ge(shiftT_copied, b + 1)
                sp.dma_start(shift_dram[b].rearrange("(k c) q -> c k q", k=2), shiftT[:]).then_inc(shift_saved, 16)
                sp.wait_ge(shift_saved, b * 16 + 16 + GRANT_DMA)
                sp.dma_start(q_stack[SHIFT_ROW:ROWS, b, :], shift_dram[b].rearrange("(k c) q -> k (c q)", k=PARTS)).then_inc(shift_loaded, 16)

            def save_heads(b, hg):
                sp.wait_ge(heads_copied, b * NHG + hg + 1 + GRANT)
                sp.dma_start(heads_dram[b, hg * P:(hg + 1) * P, :], heads_sb[:, hg % 2, :]).then_inc(heads_saved[hg % 2], 16)

            def load_sums(b):
                for s in range(2):
                    sp.wait_ge(heads_saved[s], b * 32 + 32 + GRANT_DMA)
                head = heads_dram[b].rearrange("(h r) t -> h r t", r=AUG)
                sp.dma_start(numer[:, ds(b * T, T)], head[:, 0:D, :]).then_inc(sums_loaded, 16)
                sp.dma_start(denom[:, ds(b * T, T)], head[:, D:2 * D, :]).then_inc(sums_loaded, 16)
                sp.wait_ge(sums_loaded, b * 32 + 32)

            load_shift(0)
            sp.dma_start(rows_dram[NE * REGION:NE * REGION + P, :], c_pad).then_inc(pad_saved, 16)
            with sp.Fori(1, NB - 1) as b:
                for hg in range(2):
                    save_heads(b - 1, hg)
                    stack_parts(b + 1, hg)
                load_shift(b)
                save_heads(b - 1, 2)
                save_heads(b - 1, 3)
                load_sums(b - 1)
                sp.sem_inc(go_load, 1)
            for hg in range(2):
                save_heads(NB - 2, hg)
            load_shift(NB - 1)
            for hg in range(2, NHG):
                save_heads(NB - 2, hg)
            load_sums(NB - 2)
            sp.wait_ge(pv_done, 2 * NG + GRANT)
            for w, src in enumerate((w1, w3)):
                sp.dma_start(w13[w], src.rearrange("e k n -> k e n")).then_inc(experts_loaded, 16)
            for j, (j0, nj) in enumerate(HJ):
                sp.dma_start(w2_sb[0:nj, :, j, :], w2[:, j0:j0 + nj, :].rearrange("e k n -> k e n")).then_inc(experts_loaded, 16)
            for hg in range(NHG):
                save_heads(NB - 1, hg)
            load_sums(NB - 1)

            sp.wait_ge(table_ready, 1)
            for e in range(0, NE, 2):
                row = sp.value_load(free_row[0:1, e:e + 1], min_val=e * REGION, max_val=(e + 1) * REGION - P)
                sp.dma_start(rows_dram[ds(row, P), :], c_pad).then_inc(pad_saved, 16)

            def load_block(n, k):
                row = sp.value_load(first_rows[0:1, ds(n, 1)], min_val=0, max_val=NE * REGION)
                sp.dma_start(blk[:, k, :], rows_dram[ds(row, P), :]).then_inc(blk_loaded[k], 16)

            sp.wait_ge(table_ready, 2)
            sp.wait_ge(rows_sent, 16 * 2 * NT)
            sp.wait_ge(pad_saved, 16 * (NE + 1))
            for n in range(4):
                load_block(n, n)
            with sp.Fori(1, NBLK // 4) as p:
                for k in range(4):
                    sp.wait_ge(blkT_ps, p * 4 + k - 3)
                    sp.wait_ge(where_done, p * 4 + k - 3)
                    sp.sem_inc(go_load, 1)
                    load_block(p * 4 + k, k)

            for k in range(4):
                sp.wait_ge(y_sent[k], 16 * (NBLK // 4))
            y_tok = y_dram.rearrange("(k t p) e -> k p t e", k=2, p=P)
            for b in range(NB):
                for k in range(2):
                    sp.dma_start(y_sb[:, k, tiles(b), :], y_tok[k, :, tiles(b), :]).then_inc(y_loaded[b], 16)
            for b in range(NB):
                sp.wait_ge(out_ready, b + 1)
                sp.dma_start(out_tiles[:, tiles(b), :], x_sb[:, tiles(b), :]).then_inc(out_saved, 16)
            sp.wait_ge(out_saved, 16 * NB)

        @block.gpsimd
        def _(pool):
            nc.gpsimd.memset(half[:], -0.5).then_inc(half_set, 1)
            nc.gpsimd.memset(v_aug[:, :, :, D:2 * D], 1.0).then_inc(aug_filled, 1)
            nc.gpsimd.memset(v_aug[:, :, :, 2 * D:AUG], 0.0).then_inc(aug_filled, 1)

            def deviation(b):
                pool.wait_ge(half_set, 1)
                pool.wait_ge(var_done, b + 1)
                nc.gpsimd.tensor_tensor(rstd[:, tiles(b)], veps[:, tiles(b)], half[:], ALU.pow).then_inc(rstd_done, 1)

            def normalise(b):
                deviation(b)
                pool.wait_ge(rstd_done, b + 1)
                if b:
                    pool.wait_ge(xT_ps, b)
                for j in range(QT):
                    t = b * QT + j
                    nc.gpsimd.tensor_scalar(xn[:, j], x_sb[:, t], moments[:, t, 0:1], rstd[:, t:t + 1],
                                            ALU.subtract, ALU.mult).then_inc(xn_ready, 1)

            def add_products(b, w):
                i = 2 * b + w
                pool.wait_ge(rope_read, 2 * i + 2)
                if i:
                    pool.wait_ge(rest_done, i)
                    pool.wait_ge(part0_done, i)
                nc.gpsimd.tensor_tensor(rotated, rot[:, 0], rot[:, 1], ALU.add).then_inc(sum_done, 1)

            def take_part0(b, w):
                i = 2 * b + w
                pool.wait_ge(part0_done, i + 1)
                if i:
                    pool.wait_ge(parts_ready, i)
                nc.gpsimd.tensor_tensor(rest, rotated, parts[:, w, 0], ALU.subtract).then_inc(rest_done, 1)

            def take_part1(b, w):
                i = 2 * b + w
                pool.wait_ge(part1_done, i + 1)
                pool.wait_ge(rest_done, i + 1)
                nc.gpsimd.tensor_tensor(parts[:, w, 2], rest, parts[:, w, 1], ALU.subtract).then_inc(parts_ready, 1)

            def split(b):
                add_products(b, 0)
                take_part0(b, 0)
                add_products(b, 1)
                take_part1(b, 0)
                take_part0(b, 1)
                take_part1(b, 1)

            def fill_values(b):
                pool.wait_ge(v_copied, b + 1)
                pool.wait_ge(pv_done, b * NG + GRANT)
                pool.wait_ge(aug_filled, 2)
                nc.gpsimd.tensor_copy(v_aug[:, :, :, 0:D],
                                      v_all[:, tiles(b), :].rearrange("p t (h d) -> p t h d", h=H)).then_inc(v_aug_ready, 1)

            def send_rows(b):
                pool.wait_ge(var2, b + 1)
                nc.gpsimd.tensor_tensor(rstd[:, 0:QT], veps[:, 0:QT], half[:], ALU.pow).then_inc(rstd2, 1)
                pool.wait_ge(place_ready, b + 1)
                for j in range(QT):
                    for k in range(2):
                        pool.wait_ge(rows_ready, (b * QT + j) * 2 + k + 1)
                        nc.gpsimd.indirect_dma_start(
                            out=rows_dram, out_offset=bass.IndirectOffsetOnAxis(ap=place[:, k, j:j + 1], axis=0),
                            in_=rows[:, k, j, :], in_offset=None).then_inc(rows_sent, 16)

            deviation(0)
            add_products(0, 0)
            deviation(1)
            take_part0(0, 0)
            add_products(0, 1)
            take_part1(0, 0)
            take_part0(0, 1)
            take_part1(0, 1)
            split(1)
            normalise(2)
            for b in range(NB - 2):
                fill_values(b)
                split(b + 2)
                if b + 3 < NB:
                    normalise(b + 3)
            fill_values(NB - 2)
            send_rows(0)
            fill_values(NB - 1)
            for b in range(1, NB):
                send_rows(b)

            with pool.Fori(0, NBLK // 4) as p:
                for k in range(4):
                    pool.wait_ge(where_done, p * 4 + k + 1)
                    pool.wait_ge(y_ready, p * 4 + k + 1)
                    pool.sem_inc(go_scatter, 1)
                    nc.gpsimd.indirect_dma_start(
                        out=y_dram, out_offset=bass.IndirectOffsetOnAxis(ap=where[:, k, :], axis=0),
                        in_=y_rows[:, k, :], in_offset=None, bounds_check=2 * NB * T - 1,
                        oob_is_err=False).then_inc(y_sent[k], 16)

        @block.scalar
        def _(act):
            act.sem_inc(exp_done, GRANT)
            act.sem_inc(heads_copied, GRANT)
            for dst, src in ((w_raw[0:L, 1], wk_up), (w_raw[0:L, 2], wv_up), (w_raw[:, 0], wq), (w_raw[:, 3], wo)):
                act.dma_start(dst, src).then_inc(w_loaded, 16)
            for dst, src in ((eye[:], c_eye), (rope[:].rearrange("p k t -> p (k t)"), c_rope)):
                act.dma_start(dst, src).then_inc(c_loaded, 16)
            for dst, src in ((eye16[:], c_eye16), (gw_sb[:], gate_w), (bias_sb[:], expert_bias.unsqueeze(0).to_broadcast([P, NE])),
                             (count[:], c_count), (expert[:], c_expert), (table_in[:], c_table), (dest[:], c_dest)):
                act.dma_start(dst, src).then_inc(r_loaded, 16)

            def copy_xT(b, bank):
                act.wait_ge(xT_ps, b + 1)
                if not isinstance(b, int) or b:
                    act.wait_ge(v_ps, b)
                nc.scalar.copy(xT[:], bank).then_inc(xT_copied, 1)

            def round_part0(b, w):
                act.wait_ge(sum_done, b * 2 + w + 1)
                if not isinstance(b, int) or b:
                    act.wait_ge(parts_saved[w], b * 16)
                nc.scalar.copy(parts[:, w, 0], rotated).then_inc(part0_done, 1)

            def round_part1(b, w):
                act.wait_ge(rest_done, b * 2 + w + 1)
                nc.scalar.copy(parts[:, w, 1], rest).then_inc(part1_done, 1)

            def copy_v(b):
                act.wait_ge(v_ps, b + 1)
                nc.scalar.copy(v_all[:, ds(b * QT, QT), :].rearrange("p t e -> p (t e)"), ps_m[:]).then_inc(v_copied, 1)

            for b in range(2):
                copy_xT(b, ps_o[:])
                round_part0(b, 0)
                copy_v(b)
                round_part1(b, 0)
                round_part0(b, 1)
                round_part1(b, 1)

            def copy_heads(b, hg):
                act.wait_ge(pv_done, b * NG + QT * (hg + 1) + GRANT)
                act.wait_ge(heads_saved[hg % 2], b * 32 + 16 * (hg // 2) + GRANT_DMA)
                nc.scalar.copy(heads_sb[:, hg % 2, :], ps_o[:]).then_inc(heads_copied, 1)

            def exponentials(b, g):
                n = T - P * (g % QT)
                act.wait_ge(pv_done, b * NG + max(g - 1, 0) + GRANT)
                for j in range(2):
                    act.wait_ge(scores_ready, b * NPAIR + 2 * g + j + 1)
                    nc.scalar.activation(prob[:, g % 2, 2 * j:2 * j + 2, 0:n], ps_b2[:, j, :, 0:n], ACT.Exp,
                                         scale=SCALE).then_inc(exp_done, 1)
                if g % QT == 0 and g > 0:
                    copy_heads(b, g // QT - 1)

            def copy_xn2T(b):
                act.wait_ge(xn2T_ps, b + 1)
                if b:
                    act.wait_ge(logits_done, b)
                nc.scalar.copy(xn2T, ps_m[:]).then_inc(xn2T_copied, 1)

            def exp_gate(b):
                act.wait_ge(gate_in, b + 1)
                nc.scalar.activation(route[:, 2], route[:, 1], ACT.Exp).then_inc(gate_exp, 1)

            with act.Fori(1, NB - 1) as b:
                for g in range(NG):
                    if g == 0:
                        copy_xT(b + 1, ps_m[:])
                    exponentials(b - 1, g)
                    for w in range(2):
                        if g == PART0_AT[w]:
                            round_part0(b + 1, w)
                        if g == PART1_AT[w]:
                            round_part1(b + 1, w)
                    if g == COPY_V_AT:
                        copy_v(b + 1)
                copy_heads(b - 1, NHG - 1)
            for b, routes in ((NB - 2, ROUTE_AT[0:1]), (NB - 1, ROUTE_AT[1:])):
                for g in range(NG):
                    for r, at in routes:
                        if g == at["turn"]:
                            copy_xn2T(r)
                        if g == at["gate"] + 1:
                            exp_gate(r)
                    exponentials(b, g)
                copy_heads(b, NHG - 1)
            for r, at in ROUTE_AT[1:]:
                if at["turn"] >= NG:
                    copy_xn2T(r)
                if at["gate"] + 1 >= NG:
                    exp_gate(r)
            copy_xn2T(NB - 1)
            exp_gate(NB - 1)

            act.wait_ge(table_ready, 1)
            for e in range(1, NE, 2):
                row = act.value_load(free_row[0:1, e:e + 1], min_val=e * REGION, max_val=(e + 1) * REGION - P)
                act.dma_start(rows_dram[ds(row, P), :], c_pad).then_inc(pad_saved, 16)

            def copy_blkT(n, k):
                act.wait_ge(blkT_ps, n + 1)
                if not (isinstance(n, int) and n < 2):
                    act.wait_ge(up_done, n - 1)
                nc.scalar.copy(blkT[:, k % 2, :], ps_o[:, 0:P]).then_inc(blkT_copied, 1)

            def silu(n, k):
                act.wait_ge(up_done, n + 1)
                if not (isinstance(n, int) and n < 2):
                    act.wait_ge(hid_done, n - 1)
                nc.scalar.activation(gate[:, k % 2, :], ps_b[:, 2 * (k % 2), 0:HID], ACT.Silu).then_inc(gate_done, 1)

            def copy_hidT(n, k):
                act.wait_ge(hidT_ps, n + 1)
                if not (isinstance(n, int) and n < 2):
                    act.wait_ge(down_done, n - 1)
                nj = HJ[2][1]
                nc.scalar.copy(hidT[:, k % 2, 0:2 * P], ps_a[:, k % 2, 0:2 * P]).then_inc(hidT_copied, 1)
                nc.scalar.copy(hidT[0:nj, k % 2, 2 * P:3 * P], ps_a[0:nj, k % 2, 2 * P:3 * P]).then_inc(hidT_copied, 1)

            def step(n, k, last=NBLK):
                late = not isinstance(n, int)
                if late or n + 1 < last:
                    copy_blkT(n + 1, k + 1)
                if late or n < last:
                    silu(n, k)
                if late or n >= 1:
                    copy_hidT(n - 1, k + 3)

            copy_blkT(0, 0)
            for n in range(4):
                step(n, n)
            with act.Fori(1, NBLK // 4 - 1) as p:
                for k in range(4):
                    step(p * 4 + k, k)
            for k in range(5):
                step(NBLK - 4 + k, k)

        @block.vector
        def _(dve):
            dve.sem_inc(shift_step, GRANT)
            def norm_stats(b):
                dve.wait_ge(x_loaded[b], 16)
                if b:
                    dve.wait_ge(moments_done, NT // NB * b)
                for j in range(QT):
                    nc.vector.bn_stats(stats[:, j, :], x_sb[:, b * QT + j, :]).then_inc(stats_done, 1)
                for j in range(QT):
                    t = b * QT + j
                    dve.wait_ge(stats_done, t + 1)
                    nc.vector.bn_aggr(moments[:, t, :], stats[:, j, :]).then_inc(moments_done, 1)
                dve.wait_ge(moments_done, QT * (b + 1))
                nc.vector.tensor_scalar(veps[:, tiles(b)], moments[:, tiles(b), 1], EPS, None, ALU.add).then_inc(var_done, 1)

            def permuted(i, src):
                v = src.rearrange("p (h i two) -> p i two h", i=D // 2, two=2)
                own = w_proj[:, i].rearrange("p (i two h) -> p i two h", i=D // 2, two=2)
                swapped = w_proj[:, i + 1].rearrange("p (i two h) -> p i two h", i=D // 2, two=2)
                for c in range(2):
                    nc.vector.tensor_copy(own[:, :, c], v[:, :, c]).then_inc(w_ready, 1)
                    nc.vector.tensor_copy(swapped[:, :, c], v[:, :, 1 - c]).then_inc(w_ready, 1)

            def norm(b):
                dve.wait_ge(rstd_done, b + 1)
                if b:
                    dve.wait_ge(xT_ps, b)
                for j in range(QT):
                    t = b * QT + j
                    nc.vector.tensor_scalar(xn[:, j], x_sb[:, t], moments[:, t, 0:1], rstd[:, t:t + 1],
                                            ALU.subtract, ALU.mult).then_inc(xn_ready, 1)

            norm_stats(0)
            norm(0)
            dve.wait_ge(w_loaded, 16 * 5)
            permuted(0, w_raw[:, 0])
            dve.wait_ge(wdT_ps, 1)
            nc.vector.tensor_copy(wdT[:], ps_m[0:L, 0:E]).then_inc(wdT_done, 1)
            dve.wait_ge(wkv_ps, 1)
            permuted(2, ps_m[:, 0:E])
            nc.vector.tensor_copy(w_proj[:, 4], ps_m[:, E:2 * E]).then_inc(w_ready, 1)

            def rotate(b, i, bank):
                if not (isinstance(b, int) and 2 * b + i // 2 == 0):
                    dve.wait_ge(sum_done, b * 2 + i // 2)
                dve.wait_ge(proj_done, b * 4 + i + 1)
                nc.vector.tensor_tensor(rot[:, i % 2], bank, rope[:, i % 2], ALU.mult).then_inc(rope_read, 1)

            m3 = negmax[:, :].rearrange("p (h q) -> p q h", q=QT)

            def maximum(b, n):
                qt, h, nh = MAX_UNITS[n]
                keys = P * (qt + 1)
                dve.wait_ge(max_scores, b * NMU + n + 1)
                nc.vector.tensor_reduce(m3[:, qt, h:h + nh],
                                        ps_a[:, n % 2, 0:nh * keys].rearrange("p (a k) -> p a k", a=nh),
                                        AXX, ALU.max, negate=True).then_inc(max_read, 1)

            def split_maxima(b):
                done = b * 4 + GRANT
                dve.wait_ge(max_read, b * NMU + NMU)
                if not isinstance(b, int) or b:
                    dve.wait_ge(shiftT_done, b)
                nc.vector.tensor_copy(shift[:, 0], negmax[:]).then_inc(shift_step, 1)
                dve.wait_ge(shift_step, done + 1)
                nc.vector.tensor_tensor(shift_rest[:], negmax[:], shift[:, 0], ALU.subtract).then_inc(shift_step, 1)
                dve.wait_ge(shift_step, done + 2)
                nc.vector.tensor_copy(shift[:, 1], shift_rest[:]).then_inc(shift_step, 1)
                dve.wait_ge(shift_step, done + 3)
                nc.vector.tensor_tensor(shift[:, 2], shift_rest[:], shift[:, 1], ALU.subtract).then_inc(shift_step, 1)

            def copy_shiftT(b):
                dve.wait_ge(shiftT_done, b + 1)
                dve.wait_ge(shift_saved, b * 16 + GRANT_DMA)
                nc.vector.tensor_copy(shiftT[:], shiftT_ps).then_inc(shiftT_copied, 1)

            dve.wait_ge(c_loaded, 16 * 2)
            for i in range(4):
                rotate(0, i, ps_b[:, i])
            norm_stats(1)
            norm(1)
            dve.wait_ge(gwT_ps, 1)
            nc.vector.tensor_copy(gwT[:], ps_m[:, 0:NE]).then_inc(gwT_done, 1)
            for b in range(2, NB):
                norm_stats(b)
            for i in range(4):
                rotate(1, i, ps_b[:, i])
            for n in range(NMU):
                maximum(0, n)
            split_maxima(0)
            copy_shiftT(0)
            dve.wait_ge(shift_step, 4 + GRANT)
            for n in range(AHEAD):
                maximum(1, n)
            with dve.Fori(1, NB - 1) as b:
                for what, n in pass_order(PREPARE):
                    if what == "max":
                        maximum(b, n)
                    elif what == "next max":
                        maximum(b + 1, n)
                    elif what == "rotate":
                        rotate(b + 1, n, ps_m[:])
                    elif what == "split":
                        split_maxima(b)
                        dve.wait_ge(shift_step, b * 4 + 4 + GRANT)
                    elif what == "shift":
                        copy_shiftT(b)

            dve.wait_ge(r_loaded, 16 * 7)
            per = lambda a: a.rearrange("p (t e) -> p t e", e=NE)
            over = lambda a: a.to_broadcast([P, QT, NE])
            R = [per(route[:, k]) for k in range(12)]
            largest, total, inverse = R[0][:, :, 0:1], R[0][:, :, 1:2], R[0][:, :, 2:3]
            logits = per(ps_m[:, 0:QT * NE])
            rank = per(ps_m[:, QT * NE:2 * QT * NE])
            added = ps_m[:, 2 * QT * NE:2 * QT * NE + NE]
            n_step = [0]

            def routed(instruction):
                n_step[0] += 1
                instruction.then_inc(route_step, 1)
                dve.wait_ge(route_step, n_step[0])

            def normalise_heads(t):
                cols = slice(t * P, (t + 1) * P)
                dve.wait_ge(sums_loaded, 32 * (t // QT + 1))
                nc.vector.reciprocal(denom[:, cols], denom[:, cols]).then_inc(inv_done, 1)
                dve.wait_ge(inv_done, t + 1)
                nc.vector.tensor_tensor(numer[:, cols], numer[:, cols], denom[:, cols], ALU.mult).then_inc(normed, 1)

            def add_residual(b):
                xb = x_sb[:, tiles(b), :].rearrange("p t e -> p (t e)")
                dve.wait_ge(wo_done, b + 1)
                nc.vector.tensor_tensor(xb, ps_m[:], xb, ALU.add).then_inc(x2_ready, 1)
                dve.wait_ge(x2_ready, b + 1)
                for j in range(QT):
                    nc.vector.bn_stats(stats[:, j, :], x_sb[:, b * QT + j, :]).then_inc(stats2, 1)
                dve.wait_ge(stats2, b * QT + QT)
                for j in range(QT):
                    nc.vector.bn_aggr(moments[:, j, :], stats[:, j, :]).then_inc(moments2, 1)
                dve.wait_ge(moments2, b * QT + QT)
                nc.vector.tensor_scalar(veps[:, 0:QT], moments[:, 0:QT, 1], EPS, None, ALU.add).then_inc(var2, 1)

            def second_norm(b):
                dve.wait_ge(rstd2, b + 1)
                for j in range(QT):
                    nc.vector.tensor_scalar(xn2[:, j], x_sb[:, b * QT + j, :], moments[:, j, 0:1], rstd[:, j:j + 1],
                                            ALU.subtract, ALU.mult).then_inc(xn2_ready, 1)

            def gate_input(b):
                dve.wait_ge(logits_done, b + 1)
                routed(nc.vector.tensor_reduce(largest, logits, AXX, ALU.max))
                nc.vector.tensor_tensor(R[1], logits, over(largest), ALU.subtract).then_inc(gate_in, 1)

            def choose(b):
                dve.wait_ge(gate_exp, b + 1)
                routed(nc.vector.tensor_reduce(total, R[2], AXX, ALU.add))
                routed(nc.vector.reciprocal(inverse, total))
                routed(nc.vector.tensor_tensor(R[3], R[2], over(inverse), ALU.mult))
                routed(nc.vector.tensor_tensor(R[4], R[3], bias_sb[:].unsqueeze(1).to_broadcast([P, QT, NE]), ALU.add))
                for j in range(QT):
                    nc.vector.max(R[5][:, j], R[4][:, j]).then_inc(best_found, 1)
                dve.wait_ge(best_found, b * 2 * QT + QT)
                for j in range(QT):
                    nc.vector.max_index(R[6][:, j].bitcast(U32), R[5][:, j], R[4][:, j]).then_inc(best_found, 1)
                dve.wait_ge(best_found, b * 2 * QT + 2 * QT)
                routed(nc.vector.tensor_copy(route[:, 7], route[:, 6].bitcast(U32)))
                for k in range(2):
                    routed(nc.vector.tensor_tensor(R[8 + k], expert[:, 0:1, :].to_broadcast([P, QT, NE]),
                                                   over(R[7][:, :, k:k + 1]), ALU.is_equal))
                nc.vector.tensor_tensor(taken[:], route[:, 8], route[:, 9], ALU.add).then_inc(taken_ready, 1)
                for k in range(2):
                    routed(nc.vector.tensor_tensor(R[10], R[8 + k], R[3], ALU.mult))
                    routed(nc.vector.tensor_reduce(picked[:, 0, k], R[10], AXX, ALU.add))

            def find_places(b):
                if b:
                    dve.wait_ge(rows_sent, 16 * 2 * QT * b)
                else:
                    for w in range(2):
                        dve.wait_ge(parts_saved[w], 16 * NB)
                routed(nc.vector.tensor_copy(rows[:, :, :, E].bitcast(I32), dest[:, tiles(b), :].rearrange("p t k -> p k t")))
                dve.wait_ge(ranked, b + 1)
                routed(nc.vector.tensor_tensor(R[11], rank, expert[:, 1:2, :].to_broadcast([P, QT, NE]), ALU.add))
                routed(nc.vector.tensor_tensor(expert[:, 1], expert[:, 1], added, ALU.add))
                for k in range(2):
                    routed(nc.vector.tensor_tensor(R[10], R[8 + k], R[11], ALU.mult))
                    routed(nc.vector.tensor_reduce(picked[:, 1, k], R[10], AXX, ALU.add))
                nc.vector.tensor_copy(place[:], picked[:, 1]).then_inc(place_ready, 1)
                for j in range(QT):
                    for k in range(2):
                        nc.vector.tensor_scalar(rows[:, k, j, 0:E], xn2[:, j], picked[:, 0, k, j:j + 1], None,
                                                ALU.mult).then_inc(rows_ready, 1)
                assert n_step[0] == ROUTE_STEPS * (b + 1), n_step[0]

            route_stages = {"heads": normalise_heads, "residual": add_residual, "norm": second_norm,
                            "gate": gate_input, "choose": choose, "places": find_places}
            for what, n in pass_order(ROUTE_FIRST):
                if what == "max":
                    maximum(NB - 1, n)
                elif what == "split":
                    split_maxima(NB - 1)
                elif what == "shift":
                    copy_shiftT(NB - 1)
                elif what in route_stages:
                    route_stages[what](n)
            for what, n in pass_order(ROUTE_REST, maxima=False):
                if what in route_stages:
                    route_stages[what](n)
            for t in range((NB - 1) * QT, NT):
                normalise_heads(t)
            for stage in (add_residual, second_norm, gate_input, choose, find_places):
                stage(NB - 1)

            n_table = [0]

            def tabled(instruction):
                n_table[0] += 1
                instruction.then_inc(table_step, 1)
                dve.wait_ge(table_step, n_table[0])

            n0 = NBLK * NE
            block_no = table_in[:, 0:n0].rearrange("p (n e) -> p n e", e=NE)
            up_to = table_in[:, n0:n0 + NE * NE].rearrange("p (e f) -> p e f", e=NE)
            first_row = table_in[:, n0 + NE * NE:n0 + NE * NE + NE]
            n1 = n0 + NE * NE + NE
            block_no1 = table_in[:, n1:n1 + NBLK]
            place_value = table_in[:, n1 + NBLK:].rearrange("p (k n) -> p k n", k=2)
            wide = [tables[:, k].rearrange("p (n e) -> p n e", e=NE) for k in range(2)]
            S = [short[:, k] for k in range(8)]
            e1 = lambda k: S[k][:, 0:NE]
            nc.vector.tensor_copy(free_row[:], expert[0:1, 1]).then_inc(table_ready, 1)
            tabled(nc.vector.tensor_tensor(e1(0), expert[0:1, 1], first_row, ALU.subtract))
            tabled(nc.vector.tensor_scalar(e1(1).bitcast(I32), e1(0), float(P - 1), None, ALU.add))
            tabled(nc.vector.tensor_scalar(e1(2).bitcast(I32), e1(1).bitcast(I32), P.bit_length() - 1, None, ALU.logical_shift_right))
            tabled(nc.vector.tensor_copy(e1(3), e1(2).bitcast(I32)))
            in_blocks = e1(3)
            tabled(nc.vector.tensor_tensor(wide[0][:, 0:NE], up_to, in_blocks.unsqueeze(1).to_broadcast([1, NE, NE]), ALU.mult))
            tabled(nc.vector.tensor_reduce(e1(4), wide[0][:, 0:NE], AXX, ALU.add))
            tabled(nc.vector.tensor_tensor(wide[0], block_no, e1(4).unsqueeze(1).to_broadcast([1, NBLK, NE]), ALU.is_ge))
            tabled(nc.vector.tensor_reduce(S[5], wide[0], AXX, ALU.add))
            tabled(nc.vector.tensor_tensor(wide[1], wide[0], in_blocks.unsqueeze(1).to_broadcast([1, NBLK, NE]), ALU.mult))
            tabled(nc.vector.tensor_reduce(S[6], wide[1], AXX, ALU.add))
            tabled(nc.vector.tensor_tensor(S[7], block_no1, S[6], ALU.subtract))
            tabled(nc.vector.tensor_scalar(S[0], S[5], float(NE), float(P), ALU.is_lt, ALU.mult))
            tabled(nc.vector.tensor_tensor(S[1], S[7], S[0], ALU.mult))
            tabled(nc.vector.tensor_scalar(S[2], S[5], float(REGION), None, ALU.mult))
            nc.vector.tensor_tensor(first_rows[:], S[1], S[2], ALU.add).then_inc(table_ready, 1)
            tabled(nc.vector.tensor_scalar(S[3], S[5], float(NE - 1), None, ALU.min))
            for k in range(2):
                tabled(nc.vector.tensor_tensor(S[4 + k], S[3], place_value[:, k], ALU.mult))
            for k in range(2):
                tabled(nc.vector.tensor_reduce(S[6 + k][:, 0:NQ], S[4 + k].rearrange("p (g n) -> p g n", n=4), AXX, ALU.add))
            nc.vector.tensor_copy(experts[:, 0:1], S[6][:, 0:1]).then_inc(table_ready, 1)
            nc.vector.tensor_tensor(experts[:, 1:NQ], S[6][:, 1:NQ], S[7][:, 0:NQ - 1], ALU.add).then_inc(table_ready, 1)

            def keep_where(p, k):
                dve.wait_ge(blk_loaded[k], p * 16 + 16)
                if not (isinstance(p, int) and p == 0):
                    dve.wait_ge(y_sent[k], p * 16)
                nc.vector.tensor_copy(where[:, k, :], blk[:, k, E:E + 1].bitcast(U32)).then_inc(where_done, 1)

            def product(n, k):
                dve.wait_ge(gate_done, n + 1)
                if not (isinstance(n, int) and n < 2):
                    dve.wait_ge(hidT_ps, n - 1)
                nc.vector.tensor_tensor(hid[:, k % 2, :], ps_b[:, 2 * (k % 2) + 1, 0:HID], gate[:, k % 2, :],
                                        ALU.mult).then_inc(hid_done, 1)

            def result(n, k):
                dve.wait_ge(down_done, n + 1)
                nc.vector.tensor_copy(y_rows[:, k % 4, :], ps_m[:, 0:E]).then_inc(y_ready, 1)

            def step(p, k, n_last=NBLK):
                n = p * 4 + k
                if not isinstance(n, int) or n < n_last:
                    keep_where(p, k)
                    product(n, k)
                if not isinstance(n, int) or n >= 2:
                    result(n - 2, k + 2)

            for k in range(4):
                step(0, k)
            with dve.Fori(1, NBLK // 4 - 1) as p:
                for k in range(4):
                    step(p, k)
            for k in range(6):
                step(NBLK // 4 - 1, k)

            for b in range(NB):
                dve.wait_ge(y_loaded[b], 32)
                nc.vector.tensor_tensor(x_sb[:, tiles(b), :], x_sb[:, tiles(b), :], y_sb[:, 0, tiles(b), :], ALU.add).then_inc(y_added, 1)
                dve.wait_ge(y_added, b + 1)
                nc.vector.tensor_tensor(x_sb[:, tiles(b), :], x_sb[:, tiles(b), :], y_sb[:, 1, tiles(b), :], ALU.add).then_inc(out_ready, 1)

        @block.tensor
        def _(pe):
            pe.sem_inc(pv_done, GRANT)
            pe.wait_ge(w_loaded, 16 * 5)
            pe.wait_ge(c_loaded, 16 * 2)
            nc.tensor.transpose(ps_m[0:L, 0:E], wd_sb[:], eye[:]).then_inc(wdT_ps, 1)
            pe.wait_ge(wdT_done, 1)
            nc.tensor.matmul(ps_m[:, 0:E], wdT[:], w_raw[0:L, 1], start=True, stop=True)
            nc.tensor.matmul(ps_m[:, E:2 * E], wdT[:], w_raw[0:L, 2], start=True, stop=True).then_inc(wkv_ps, 1)
            pe.wait_ge(w_ready, 9)

            def turn_x(b, bank):
                pe.wait_ge(xn_ready, b * QT + QT)
                if not isinstance(b, int):
                    pe.wait_ge(shiftT_copied, b - 1)
                elif b:
                    pe.wait_ge(xT_copied, b)
                for j in range(QT):
                    last = nc.tensor.transpose(bank[:, j * P:(j + 1) * P], xn[:, j, :], eye[:])
                last.then_inc(xT_ps, 1)

            def project(b, i, bank):
                pe.wait_ge(xT_copied, b + 1)
                if not isinstance(b, int):
                    if i:
                        pe.wait_ge(rope_read, b * 4 + i)
                elif b:
                    pe.wait_ge(rope_read, 4 * (b - 1) + i + 1)
                nc.tensor.matmul(bank, w_proj[:, i], xT[:], start=True, stop=True).then_inc(proj_done, 1)

            def project_v(b):
                if not isinstance(b, int):
                    pe.wait_ge(rope_read, b * 4 + 4)
                elif b:
                    pe.wait_ge(gwT_done, 1)
                for j in range(QT):
                    last = nc.tensor.matmul(ps_m[:, j * P:(j + 1) * P], xT[:, j * P:(j + 1) * P], w_proj[:, 4], start=True, stop=True)
                last.then_inc(v_ps, 1)

            def qs(b, h, t0, n, rows):
                return q_stack[0:rows, b, h * T + t0:h * T + t0 + n]

            def ks(b, h, t0, n, rows):
                return k_stack[0:rows, b, h * T + t0:h * T + t0 + n]

            def max_unit(b, n):
                qt, h0, nh = MAX_UNITS[n]
                keys = P * (qt + 1)
                if not (isinstance(b, int) and b * NMU + n < 2):
                    pe.wait_ge(max_read, b * NMU + n - 1)
                for a in range(nh):
                    last = nc.tensor.matmul(ps_a[:, n % 2, a * keys:(a + 1) * keys], qs(b, h0 + a, qt * P, P, SHIFT_ROW),
                                            ks(b, h0 + a, 0, keys, SHIFT_ROW), start=True, stop=True)
                last.then_inc(max_scores, 1)

            def transpose_shift(b):
                pe.wait_ge(shift_step, b * 4 + 4 + GRANT)
                if isinstance(b, int) and b == NB - 1:
                    pe.wait_ge(route_step, ROUTE_STEPS)
                else:
                    pe.wait_ge(v_copied, b + 2)
                for k in range(2):
                    last = nc.tensor.transpose(shiftT_ps[:, k, :], shift_cols[:, k * SR:(k + 1) * SR], eye16[:])
                last.then_inc(shiftT_done, 1)

            def scores(b, g, j):
                hg, kt = divmod(g, QT)
                if g == 0 and j == 0:
                    pe.wait_ge(shift_loaded, b * 16 + 16)
                u = 2 * g + j
                pe.wait_ge(exp_done, b * NPAIR + max(u - 1, 0) + GRANT)
                for a in range(2):
                    h = HG * hg + 2 * j + a
                    last = nc.tensor.matmul(ps_b2[:, j, a, 0:T - kt * P], ks(b, h, kt * P, P, ROWS),
                                            qs(b, h, kt * P, T - kt * P, ROWS), start=True, stop=True)
                last.then_inc(scores_ready, 1)

            def values(b, g):
                hg, kt = divmod(g, QT)
                pe.wait_ge(exp_done, b * NPAIR + 2 * g + 2 + GRANT)
                if g == 0:
                    pe.wait_ge(v_aug_ready, b + 1)
                if kt == 0:
                    pe.wait_ge(heads_copied, b * NHG + hg + GRANT)
                for a in range(HG):
                    last = nc.tensor.matmul(ps_o[a * AUG:(a + 1) * AUG, kt * P:T], v_aug[:, kt, HG * hg + a, :],
                                            prob[:, g % 2, a, 0:T - kt * P], start=kt == 0, stop=kt == QT - 1)
                last.then_inc(pv_done, 1)

            for b in range(2):
                turn_x(b, ps_o)
                for i in range(4):
                    project(b, i, ps_b[:, i])
                project_v(b)
                if b == 0:
                    pe.wait_ge(r_loaded, 16 * 7)
                    pe.wait_ge(v_copied, 1)
                    nc.tensor.transpose(ps_m[:, 0:NE], gw_sb[:], eye[0:NE, 0:NE]).then_inc(gwT_ps, 1)
            pe.wait_ge(rows_loaded, 16 * 2 * NB)
            pe.wait_ge(stack0_loaded, STACK_DMAS)
            for n in range(NMU):
                max_unit(0, n)
            transpose_shift(0)
            pe.wait_ge(rope_read, 4 * 2)
            pe.wait_ge(stack_loaded, STACK_DMAS)
            for n in range(AHEAD):
                max_unit(1, n)
            with pe.Fori(1, NB - 1) as b:
                for what, n in pass_order(PREPARE):
                    if what == "max":
                        max_unit(b, n)
                    elif what == "next max":
                        if n == 0:
                            pe.wait_ge(stack_loaded, b * STACK_DMAS + STACK_DMAS)
                        max_unit(b + 1, n)
                    elif what == "scores":
                        scores(b - 1, n // 2, n % 2)
                    elif what == "values":
                        values(b - 1, n)
                    elif what == "x":
                        turn_x(b + 1, ps_m)
                    elif what == "project":
                        project(b + 1, n, ps_m[:])
                    elif what == "v":
                        project_v(b + 1)
                    elif what == "shift":
                        transpose_shift(b)

            def out_project(b):
                if b:
                    pe.wait_ge(route_step, b * ROUTE_STEPS)
                pe.wait_ge(shiftT_copied, NB if b else NB - 1)
                for j in range(QT):
                    pe.wait_ge(normed, b * QT + j + 1)
                    last = nc.tensor.matmul(ps_m[:, j * P:(j + 1) * P], numer[:, (b * QT + j) * P:(b * QT + j + 1) * P],
                                            w_raw[:, 3], start=True, stop=True)
                last.then_inc(wo_done, 1)

            def turn_xn2(b):
                pe.wait_ge(xn2_ready, QT * (b + 1))
                for j in range(QT):
                    last = nc.tensor.transpose(ps_m[:, j * P:(j + 1) * P], xn2[:, j, :], eye[:])
                last.then_inc(xn2T_ps, 1)

            def gate_logits(b):
                pe.wait_ge(xn2T_copied, b + 1)
                for j in range(QT):
                    last = nc.tensor.matmul(ps_m[:, j * NE:(j + 1) * NE], xn2T[:, j * P:(j + 1) * P], gwT[:], start=True, stop=True)
                last.then_inc(logits_done, 1)

            def ranks(b):
                pe.wait_ge(taken_ready, b + 1)
                r0, n = QT * NE, QT * NE
                for i in range(QT):
                    here = ps_m[:, r0 + i * NE:r0 + (i + 1) * NE]
                    nc.tensor.matmul(here, count[:, 0], taken[:, i * NE:(i + 1) * NE], start=True, stop=(i == 0))
                    for j in range(i):
                        nc.tensor.matmul(here, count[:, 1], taken[:, j * NE:(j + 1) * NE], start=False, stop=(j == i - 1))
                for j in range(QT):
                    last = nc.tensor.matmul(ps_m[:, r0 + n:r0 + n + NE], count[:, 1], taken[:, j * NE:(j + 1) * NE],
                                            start=(j == 0), stop=(j == QT - 1))
                last.then_inc(ranked, 1)

            route_stages = {"out": out_project, "turn": turn_xn2, "logits": gate_logits, "ranks": ranks}
            for what, n in pass_order(ROUTE_FIRST):
                if what == "max":
                    max_unit(NB - 1, n)
                elif what == "scores":
                    scores(NB - 2, n // 2, n % 2)
                elif what == "values":
                    values(NB - 2, n)
                elif what == "shift":
                    transpose_shift(NB - 1)
                elif what in route_stages:
                    route_stages[what](n)
            for what, n in pass_order(ROUTE_REST, maxima=False):
                if what == "scores":
                    scores(NB - 1, n // 2, n % 2)
                elif what == "values":
                    values(NB - 1, n)
                elif what in route_stages:
                    route_stages[what](n)
            for stage in (out_project, turn_xn2, gate_logits, ranks):
                stage(NB - 1)

            def turn_blk(n, k):
                if isinstance(n, int) and n < 4:
                    pe.wait_ge(blk_loaded[k % 4], 16)
                elif isinstance(n, int):
                    pe.wait_ge(blk_loaded[k % 4], 16 * (n // 4 + 1))
                else:
                    pe.wait_ge(blk_loaded[k % 4], n * 4 - (k % 4) * 4 + 16)
                if not (isinstance(n, int) and n == 0):
                    pe.wait_ge(blkT_copied, n)
                nc.tensor.transpose(ps_o[:, 0:P], blk[:, k % 4, 0:E], eye[:]).then_inc(blkT_ps, 1)

            def experts_of(p):
                packed = pe.value_load(experts[0:1, ds(p, 1)], min_val=0, max_val=NE ** 6 - 1)
                return [(packed >> 3 * i) & (NE - 1) for i in range(6)]

            def up(n, k, e):
                pe.wait_ge(blkT_copied, n + 1)
                if not (isinstance(n, int) and n < 2):
                    pe.wait_ge(gate_done, n - 1)
                    pe.wait_ge(hid_done, n - 1)
                for w in range(2):
                    last = nc.tensor.matmul(ps_b[:, 2 * (k % 2) + w, 0:HID], blkT[:, k % 2, :], w13[w][:, ds(e, 1), :],
                                            start=True, stop=True)
                last.then_inc(up_done, 1)

            def turn_hid(n, k):
                pe.wait_ge(hid_done, n + 1)
                if not (isinstance(n, int) and n < 2):
                    pe.wait_ge(hidT_copied, n * 2 - 2)
                for j, (j0, nj) in enumerate(HJ):
                    last = nc.tensor.transpose(ps_a[0:nj, k % 2, j * P:(j + 1) * P], hid[:, k % 2, j0:j0 + nj], eye[:])
                last.then_inc(hidT_ps, 1)

            def down(n, k, e):
                pe.wait_ge(hidT_copied, n * 2 + 2)
                if not (isinstance(n, int) and n == 0):
                    pe.wait_ge(y_ready, n)
                for j, (j0, nj) in enumerate(HJ):
                    last = nc.tensor.matmul(ps_m[:, 0:E], hidT[0:nj, k % 2, j * P:(j + 1) * P], w2_sb[0:nj, ds(e, 1), j, :],
                                            start=(j == 0), stop=(j == 2))
                last.then_inc(down_done, 1)

            def step(n, k, e, last=NBLK):
                late = not isinstance(n, int)
                if late or n + 1 < last:
                    turn_blk(n + 1, k + 1)
                if late or n < last:
                    up(n, k, e[k + 2])
                if late or 1 <= n <= last:
                    turn_hid(n - 1, k + 3)
                if late or n >= 2:
                    down(n - 2, k + 2, e[k])

            pe.wait_ge(experts_loaded, 16 * 5)
            pe.wait_ge(table_ready, 4)
            turn_blk(0, 0)
            e = experts_of(0)
            for n in range(4):
                step(n, n, e)
            with pe.Fori(1, NQ - 1) as p:
                e = experts_of(p)
                for k in range(4):
                    step(p * 4 + k, k, e)
            e = experts_of(NQ - 1)
            for k in range(6):
                step(NBLK - 4 + k, k, e)


AHEAD = 8
MAX_PER_STEP = (4, 3, 2, 2)
assert NHG * sum(MAX_PER_STEP) == NMU
SHIFT_AT = 13
PREPARE = [("x", 0, 0)] + [(what, i, i + 1) for i in range(4) for what in ("project", "rotate")] + [("v", 0, 5), ("shift", 0, SHIFT_AT)]
PART0_AT, PART1_AT, COPY_V_AT = (3, 5), (4, 6), 7


def route_at(b, heads, out, residual, norm, turn, logits, gate, choose, ranks, places):
    return b, dict(heads=heads, out=out, residual=residual, norm=norm, turn=turn, logits=logits, gate=gate,
                   choose=choose, ranks=ranks, places=places)


ROUTE_AT = [route_at(0, (0, 1, 2, 3), 4, 4, 5, 6, 7, 7, 8, 10, 11),
            route_at(1, (0, 0, 0, 0), 1, 1, 2, 4, 5, 5, 6, 8, 8),
            route_at(2, (3, 3, 3, 3), 10, 10, 11, 13, 14, 14, 15, 16, 16)]


def route_stages_of(routes):
    return [entry for b, stages in routes for what, at in stages.items()
            for entry in ([(what, QT * b + j, at[j]) for j in range(QT)] if what == "heads" else [(what, b, at)])]


ROUTE_FIRST = route_stages_of(ROUTE_AT[0:1]) + [("shift", 0, SHIFT_AT)]
ROUTE_REST = route_stages_of(ROUTE_AT[1:])


def pass_order(stages, maxima=True):
    order, unit = [], AHEAD

    def maximum():
        nonlocal unit
        order.append(("max", unit) if unit < NMU else ("next max", unit - NMU))
        unit += 1
        if unit == NMU:
            order.append(("split", 0))

    for g in range(NG):
        left = MAX_PER_STEP[g % QT] if maxima else 0
        if left:
            maximum()
        order += [(what, which) for what, which, at in stages if at == g]
        for j in range(2):
            order.append(("scores", 2 * g + j))
            if left > 1 + j:
                maximum()
        if g:
            order.append(("values", g - 1))
        if left > 3:
            maximum()
    order.append(("values", NG - 1))
    return order + [(what, which) for what, which, at in stages if at >= NG]


ROUTE_STEPS = 5 + 1 + 2 + 4 + 1 + 2 + 4
STACK_DMAS = 16 * 2 * PARTS

_INS = ["L0_attn_x", "L0_attn_wq", "L0_attn_w_down", "L0_attn_wk_up", "L0_attn_wv_up", "L0_attn_wo",
        "L0_ffn_gate_w", "L0_ffn_expert_bias", "L0_ffn_w1", "L0_ffn_w2", "L0_ffn_w3"]


def kernel(**inputs):
    import concourse.bacc as bacc
    from concourse.bass_utils import run_bass_kernel_spmd

    nc = bacc.Bacc("TRN2", target_bir_lowering=False, num_devices=1)
    arrays, args = {}, []
    for name in _INS:
        a = np.ascontiguousarray(inputs[name])
        arrays[name] = a
        args.append(nc.dram_tensor(name, a.shape, mybir.dt.from_np(a.dtype), kind="ExternalInput").ap())
    out = nc.dram_tensor("out", (NB, T, E), F32, kind="ExternalOutput").ap()
    consts = {}
    for name, a in constants().items():
        arrays[name] = a
        consts[name] = nc.dram_tensor(name, a.shape, mybir.dt.from_np(a.dtype), kind="ExternalInput").ap()
    build_block(nc, *args, out, **consts)
    r = run_bass_kernel_spmd(nc, [arrays], core_ids=[0])
    return r.results[0]["out"]
```
